# Optimizing a Trainium2 kernel written in Bass

```python
import numpy as np
import jax
import jax.numpy as jnp

def _softmax(x, axis=-1):
    return jax.nn.softmax(x, axis=axis)

def _gelu(x):
    return jax.nn.gelu(x, approximate=True)

def _silu(x):
    return jax.nn.silu(x)

def _sigmoid(x):
    return jax.nn.sigmoid(x)

def _layernorm(x, axis=-1, eps=1e-05):
    m = jnp.mean(x, axis=axis, keepdims=True)
    v = jnp.var(x, axis=axis, keepdims=True)
    return (x - m) / jnp.sqrt(v + eps)

def _scatter_add(tgt, idx, src, axis=0):
    return tgt.at[idx].add(src)

def _segment_sum(src, seg, n):
    return jax.ops.segment_sum(src, seg, n)
kernel_name = 'mk_macaron_d1_jaxref_r8_39437a'

def setup_inputs(seed: int=0):
    np.random.seed(seed)
    _w = jnp.asarray

    def _L0_attn_setup():
        import jax, jax.numpy as jnp
        import numpy as np
        B, L, D, N = (4, 256, 128, 16)

        def _layernorm(x, g, b, eps=1e-05):
            mu = jnp.mean(x, axis=-1, keepdims=True)
            var = jnp.mean(jnp.square(x - mu), axis=-1, keepdims=True)
            return (x - mu) * jax.lax.rsqrt(var + eps) * g + b

        def _silu(x):
            return x * jax.nn.sigmoid(x)

        def _depthwise_conv(x, w):
            xc = x.transpose(0, 2, 1)
            y = jax.lax.conv_general_dilated(xc, w, window_strides=(1,), padding=[(1, 1)], feature_group_count=xc.shape[1], dimension_numbers=('NCH', 'OIH', 'NCH'))
            return y.transpose(0, 2, 1)

        def _selective_scan(u, A_log, D_skip, W_dt, b_dt, W_B, W_C):
            A = -jnp.exp(A_log)
            dt = jax.nn.softplus(u @ W_dt + b_dt)
            Bt = u @ W_B
            Ct = u @ W_C

            def step(h, inp):
                dt_t, B_t, C_t, u_t = inp
                dA = jnp.exp(dt_t[..., None] * A)
                h = dA * h + (dt_t * u_t)[..., None] * B_t[:, None, :]
                y = jnp.einsum('bdn,bn->bd', h, C_t)
                return (h, y)
            h0 = jnp.zeros((u.shape[0], u.shape[2], A.shape[1]), u.dtype)
            xs = (dt.transpose(1, 0, 2), Bt.transpose(1, 0, 2), Ct.transpose(1, 0, 2), u.transpose(1, 0, 2))
            _, ys = jax.lax.scan(step, h0, xs)
            return ys.transpose(1, 0, 2) + u * D_skip
        key = jax.random.key(seed)
        ks = jax.random.split(key, 12)
        s = 1.0 / np.sqrt(D)
        inp = {'x': jax.random.normal(ks[0], (B, L, D), jnp.float32), 'ln_g': jnp.ones((D,), jnp.float32), 'ln_b': jnp.zeros((D,), jnp.float32), 'w1_w': jax.random.normal(ks[1], (D, D), jnp.float32) * s, 'w1_b': jnp.zeros((D,), jnp.float32), 'v1_w': jax.random.normal(ks[2], (D, D), jnp.float32) * s, 'v1_b': jnp.zeros((D,), jnp.float32), 'w2_w': jax.random.normal(ks[3], (D, D), jnp.float32) * s, 'w2_b': jnp.zeros((D,), jnp.float32), 'conv_w': jax.random.normal(ks[4], (D, 1, 3), jnp.float32) * (1.0 / np.sqrt(3.0)), 'A_log': jnp.log(jnp.broadcast_to(jnp.arange(1, N + 1, dtype=jnp.float32), (D, N))), 'D_skip': jnp.ones((D,), jnp.float32), 'W_dt': jax.random.normal(ks[5], (D, D), jnp.float32) * (s * 0.1), 'b_dt': jnp.full((D,), -4.0, jnp.float32), 'W_B': jax.random.normal(ks[6], (D, N), jnp.float32) * s, 'W_C': jax.random.normal(ks[7], (D, N), jnp.float32) * s}
        return inp
    _L0_attn_in = _L0_attn_setup()

    def _L0_ffn_setup():
        import jax, jax.numpy as jnp
        import numpy as np
        DIM = 128
        DEPTH = 6
        HEADS = 16
        DIM_HEAD = 64
        WINDOW = 32
        INNER = HEADS * DIM_HEAD
        DIM_INNER = int(DIM * 4 * 2 / 3)
        QK_SCALE = 8.0

        def shift_tokens(t):
            a, s = jnp.split(t, 2, -1)
            s = jnp.pad(s, ((0, 0), (1, 0), (0, 0)))[:, :-1]
            return jnp.concatenate([a, s], -1)

        def l2norm(t):
            return t / jnp.maximum(jnp.linalg.norm(t, axis=-1, keepdims=True), 1e-12)

        def rotate_half(x):
            x1, x2 = jnp.split(x, 2, -1)
            return jnp.concatenate([-x2, x1], -1)

        def rotary_tables(n):
            half = jnp.arange(0, DIM_HEAD, 2, dtype=jnp.float32)
            inv_freq = 1.0 / 10000.0 ** (half / DIM_HEAD)
            t = jnp.arange(n, dtype=jnp.float32)
            freqs = t[:, None] * inv_freq[None, :]
            freqs = jnp.concatenate([freqs, freqs], -1)
            base_scale = (half + 0.4 * DIM_HEAD) / (1.4 * DIM_HEAD)
            power = (t - n // 2) / (WINDOW // 2)
            scale = base_scale[None, :] ** power[:, None]
            scale = jnp.concatenate([scale, scale], -1)
            return (freqs, scale)

        def local_attention(q, k, v):
            b, h, n, d = q.shape
            w = WINDOW
            nw = n // w
            bq = q.reshape(b, h, nw, w, d)
            bk = k.reshape(b, h, nw, w, d)
            bv = v.reshape(b, h, nw, w, d)

            def look(t):
                p = jnp.pad(t, ((0, 0), (0, 0), (1, 0), (0, 0), (0, 0)))
                return jnp.concatenate([p[:, :, :nw], p[:, :, 1:]], axis=3)
            bk2, bv2 = (look(bk), look(bv))
            seq = jnp.arange(n).reshape(nw, w)
            seq_p = jnp.pad(seq, ((1, 0), (0, 0)), constant_values=-1)
            jt = jnp.concatenate([seq_p[:nw], seq_p[1:]], axis=1)
            it = seq[:, :, None]
            jb = jt[:, None, :]
            mask = (it < jb) | (it > jb + w) | (jb == -1)
            sim = jnp.einsum('bhwie,bhwje->bhwij', bq, bk2) * QK_SCALE
            sim = jnp.where(mask, -jnp.finfo(sim.dtype).max, sim)
            attn = jax.nn.softmax(sim, -1)
            out = jnp.einsum('bhwij,bhwje->bhwie', attn, bv2)
            return out.reshape(b, h, n, d)

        def attn_layer(x, Wqkv, qs, ksc, Wo):
            b, n, _ = x.shape
            qkv = x @ Wqkv
            q, k, v = jnp.split(qkv, 3, -1)
            sh = lambda t: t.reshape(b, n, HEADS, DIM_HEAD).transpose(0, 2, 1, 3)
            q, k, v = (sh(q), sh(k), sh(v))
            q = l2norm(q) * qs
            k = l2norm(k) * ksc
            freqs, scale = rotary_tables(n)
            cos, sin = (jnp.cos(freqs), jnp.sin(freqs))
            q = q * cos * scale + rotate_half(q) * sin * scale
            inv = 1.0 / scale
            k = k * cos * inv + rotate_half(k) * sin * inv
            out = local_attention(q, k, v)
            out = out.transpose(0, 2, 1, 3).reshape(b, n, INNER)
            return out @ Wo

        def ffn_layer(x, g, bln, W1, b1, W2, b2):
            mu = x.mean(-1, keepdims=True)
            var = ((x - mu) ** 2).mean(-1, keepdims=True)
            xn = (x - mu) / jnp.sqrt(var + 1e-05) * g + bln
            hg = xn @ W1 + b1
            a, gate = jnp.split(hg, 2, -1)
            return a * jax.nn.gelu(gate, approximate=False) @ W2 + b2
        key = jax.random.key(seed)
        ks = jax.random.split(key, 8)
        B, N = (2, 256)
        init = lambda k, shape: jax.random.normal(k, shape, jnp.float32) * 0.02
        return {'x': jax.random.normal(ks[0], (B, N, DIM), jnp.float32), 'Wqkv': init(ks[1], (DEPTH, DIM, 3 * INNER)), 'q_scale': jnp.ones((DEPTH, DIM_HEAD), jnp.float32), 'k_scale': jnp.ones((DEPTH, DIM_HEAD), jnp.float32), 'Wo': init(ks[2], (DEPTH, INNER, DIM)), 'ln_g': jnp.ones((DEPTH, DIM), jnp.float32), 'ln_b': jnp.zeros((DEPTH, DIM), jnp.float32), 'W1': init(ks[3], (DEPTH, DIM, 2 * DIM_INNER)), 'b1': jnp.zeros((DEPTH, 2 * DIM_INNER), jnp.float32), 'W2': init(ks[4], (DEPTH, DIM_INNER, DIM)), 'b2': jnp.zeros((DEPTH, DIM), jnp.float32)}
    _L0_ffn_in = _L0_ffn_setup()
    _d = {'L0_attn_x': _L0_attn_in['x'], 'L0_attn_ln_g': _L0_attn_in['ln_g'], 'L0_attn_ln_b': _L0_attn_in['ln_b'], 'L0_attn_w1_w': _L0_attn_in['w1_w'], 'L0_attn_w1_b': _L0_attn_in['w1_b'], 'L0_attn_v1_w': _L0_attn_in['v1_w'], 'L0_attn_v1_b': _L0_attn_in['v1_b'], 'L0_attn_w2_w': _L0_attn_in['w2_w'], 'L0_attn_w2_b': _L0_attn_in['w2_b'], 'L0_attn_conv_w': _L0_attn_in['conv_w'], 'L0_attn_A_log': _L0_attn_in['A_log'], 'L0_attn_D_skip': _L0_attn_in['D_skip'], 'L0_attn_W_dt': _L0_attn_in['W_dt'], 'L0_attn_b_dt': _L0_attn_in['b_dt'], 'L0_attn_W_B': _L0_attn_in['W_B'], 'L0_attn_W_C': _L0_attn_in['W_C'], 'L0_ffn_Wqkv': _L0_ffn_in['Wqkv'], 'L0_ffn_q_scale': _L0_ffn_in['q_scale'], 'L0_ffn_k_scale': _L0_ffn_in['k_scale'], 'L0_ffn_Wo': _L0_ffn_in['Wo'], 'L0_ffn_ln_g': _L0_ffn_in['ln_g'], 'L0_ffn_ln_b': _L0_ffn_in['ln_b'], 'L0_ffn_W1': _L0_ffn_in['W1'], 'L0_ffn_b1': _L0_ffn_in['b1'], 'L0_ffn_W2': _L0_ffn_in['W2'], 'L0_ffn_b2': _L0_ffn_in['b2']}
    _x0 = _d['L0_attn_x']
    _d['L0_attn_x'] = jax.random.normal(jax.random.fold_in(jax.random.key(seed), 1), (8, 256, 128), dtype=_x0.dtype)
    del _x0
    return _d

def reference(L0_attn_x, L0_attn_ln_g, L0_attn_ln_b, L0_attn_w1_w, L0_attn_w1_b, L0_attn_v1_w, L0_attn_v1_b, L0_attn_w2_w, L0_attn_w2_b, L0_attn_conv_w, L0_attn_A_log, L0_attn_D_skip, L0_attn_W_dt, L0_attn_b_dt, L0_attn_W_B, L0_attn_W_C, L0_ffn_Wqkv, L0_ffn_q_scale, L0_ffn_k_scale, L0_ffn_Wo, L0_ffn_ln_g, L0_ffn_ln_b, L0_ffn_W1, L0_ffn_b1, L0_ffn_W2, L0_ffn_b2):

    def _L0_attn_ref(x, ln_g, ln_b, w1_w, w1_b, v1_w, v1_b, w2_w, w2_b, conv_w, A_log, D_skip, W_dt, b_dt, W_B, W_C):
        import jax, jax.numpy as jnp
        import numpy as np
        B, L, D, N = (4, 256, 128, 16)

        def _layernorm(x, g, b, eps=1e-05):
            mu = jnp.mean(x, axis=-1, keepdims=True)
            var = jnp.mean(jnp.square(x - mu), axis=-1, keepdims=True)
            return (x - mu) * jax.lax.rsqrt(var + eps) * g + b

        def _silu(x):
            return x * jax.nn.sigmoid(x)

        def _depthwise_conv(x, w):
            xc = x.transpose(0, 2, 1)
            y = jax.lax.conv_general_dilated(xc, w, window_strides=(1,), padding=[(1, 1)], feature_group_count=xc.shape[1], dimension_numbers=('NCH', 'OIH', 'NCH'))
            return y.transpose(0, 2, 1)

        def _selective_scan(u, A_log, D_skip, W_dt, b_dt, W_B, W_C):
            A = -jnp.exp(A_log)
            dt = jax.nn.softplus(u @ W_dt + b_dt)
            Bt = u @ W_B
            Ct = u @ W_C

            def step(h, inp):
                dt_t, B_t, C_t, u_t = inp
                dA = jnp.exp(dt_t[..., None] * A)
                h = dA * h + (dt_t * u_t)[..., None] * B_t[:, None, :]
                y = jnp.einsum('bdn,bn->bd', h, C_t)
                return (h, y)
            h0 = jnp.zeros((u.shape[0], u.shape[2], A.shape[1]), u.dtype)
            xs = (dt.transpose(1, 0, 2), Bt.transpose(1, 0, 2), Ct.transpose(1, 0, 2), u.transpose(1, 0, 2))
            _, ys = jax.lax.scan(step, h0, xs)
            return ys.transpose(1, 0, 2) + u * D_skip
        x_norm = _layernorm(x, ln_g, ln_b)
        x1 = x_norm @ w1_w + w1_b
        x_conv = _silu(_depthwise_conv(x1, conv_w))
        x_ssm = _selective_scan(x_conv, A_log, D_skip, W_dt, b_dt, W_B, W_C)
        v = _silu(x_norm @ v1_w + v1_b)
        return x_ssm * v @ w2_w + w2_b

    def _L0_ffn_ref(x, Wqkv, q_scale, k_scale, Wo, ln_g, ln_b, W1, b1, W2, b2):
        import jax, jax.numpy as jnp
        import numpy as np
        DIM = 128
        DEPTH = 6
        HEADS = 16
        DIM_HEAD = 64
        WINDOW = 32
        INNER = HEADS * DIM_HEAD
        DIM_INNER = int(DIM * 4 * 2 / 3)
        QK_SCALE = 8.0

        def shift_tokens(t):
            a, s = jnp.split(t, 2, -1)
            s = jnp.pad(s, ((0, 0), (1, 0), (0, 0)))[:, :-1]
            return jnp.concatenate([a, s], -1)

        def l2norm(t):
            return t / jnp.maximum(jnp.linalg.norm(t, axis=-1, keepdims=True), 1e-12)

        def rotate_half(x):
            x1, x2 = jnp.split(x, 2, -1)
            return jnp.concatenate([-x2, x1], -1)

        def rotary_tables(n):
            half = jnp.arange(0, DIM_HEAD, 2, dtype=jnp.float32)
            inv_freq = 1.0 / 10000.0 ** (half / DIM_HEAD)
            t = jnp.arange(n, dtype=jnp.float32)
            freqs = t[:, None] * inv_freq[None, :]
            freqs = jnp.concatenate([freqs, freqs], -1)
            base_scale = (half + 0.4 * DIM_HEAD) / (1.4 * DIM_HEAD)
            power = (t - n // 2) / (WINDOW // 2)
            scale = base_scale[None, :] ** power[:, None]
            scale = jnp.concatenate([scale, scale], -1)
            return (freqs, scale)

        def local_attention(q, k, v):
            b, h, n, d = q.shape
            w = WINDOW
            nw = n // w
            bq = q.reshape(b, h, nw, w, d)
            bk = k.reshape(b, h, nw, w, d)
            bv = v.reshape(b, h, nw, w, d)

            def look(t):
                p = jnp.pad(t, ((0, 0), (0, 0), (1, 0), (0, 0), (0, 0)))
                return jnp.concatenate([p[:, :, :nw], p[:, :, 1:]], axis=3)
            bk2, bv2 = (look(bk), look(bv))
            seq = jnp.arange(n).reshape(nw, w)
            seq_p = jnp.pad(seq, ((1, 0), (0, 0)), constant_values=-1)
            jt = jnp.concatenate([seq_p[:nw], seq_p[1:]], axis=1)
            it = seq[:, :, None]
            jb = jt[:, None, :]
            mask = (it < jb) | (it > jb + w) | (jb == -1)
            sim = jnp.einsum('bhwie,bhwje->bhwij', bq, bk2) * QK_SCALE
            sim = jnp.where(mask, -jnp.finfo(sim.dtype).max, sim)
            attn = jax.nn.softmax(sim, -1)
            out = jnp.einsum('bhwij,bhwje->bhwie', attn, bv2)
            return out.reshape(b, h, n, d)

        def attn_layer(x, Wqkv, qs, ksc, Wo):
            b, n, _ = x.shape
            qkv = x @ Wqkv
            q, k, v = jnp.split(qkv, 3, -1)
            sh = lambda t: t.reshape(b, n, HEADS, DIM_HEAD).transpose(0, 2, 1, 3)
            q, k, v = (sh(q), sh(k), sh(v))
            q = l2norm(q) * qs
            k = l2norm(k) * ksc
            freqs, scale = rotary_tables(n)
            cos, sin = (jnp.cos(freqs), jnp.sin(freqs))
            q = q * cos * scale + rotate_half(q) * sin * scale
            inv = 1.0 / scale
            k = k * cos * inv + rotate_half(k) * sin * inv
            out = local_attention(q, k, v)
            out = out.transpose(0, 2, 1, 3).reshape(b, n, INNER)
            return out @ Wo

        def ffn_layer(x, g, bln, W1, b1, W2, b2):
            mu = x.mean(-1, keepdims=True)
            var = ((x - mu) ** 2).mean(-1, keepdims=True)
            xn = (x - mu) / jnp.sqrt(var + 1e-05) * g + bln
            hg = xn @ W1 + b1
            a, gate = jnp.split(hg, 2, -1)
            return a * jax.nn.gelu(gate, approximate=False) @ W2 + b2
        for i in range(DEPTH):
            x = attn_layer(shift_tokens(x), Wqkv[i], q_scale[i], k_scale[i], Wo[i]) + x
            x = ffn_layer(shift_tokens(x), ln_g[i], ln_b[i], W1[i], b1[i], W2[i], b2[i]) + x
        return x
    x = L0_attn_x
    x = x + 0.5 * _L0_ffn_ref(_layernorm(x, axis=-1), L0_ffn_Wqkv, L0_ffn_q_scale, L0_ffn_k_scale, L0_ffn_Wo, L0_ffn_ln_g, L0_ffn_ln_b, L0_ffn_W1, L0_ffn_b1, L0_ffn_W2, L0_ffn_b2)
    x = x + _L0_attn_ref(_layernorm(x, axis=-1), L0_attn_ln_g, L0_attn_ln_b, L0_attn_w1_w, L0_attn_w1_b, L0_attn_v1_w, L0_attn_v1_b, L0_attn_w2_w, L0_attn_w2_b, L0_attn_conv_w, L0_attn_A_log, L0_attn_D_skip, L0_attn_W_dt, L0_attn_b_dt, L0_attn_W_B, L0_attn_W_C)
    x = x + 0.5 * _L0_ffn_ref(_layernorm(x, axis=-1), L0_ffn_Wqkv, L0_ffn_q_scale, L0_ffn_k_scale, L0_ffn_Wo, L0_ffn_ln_g, L0_ffn_ln_b, L0_ffn_W1, L0_ffn_b1, L0_ffn_W2, L0_ffn_b2)
    return x

_drawn_inputs = setup_inputs


def setup_inputs(seed=0):
    import zlib

    import numpy as np

    out = dict(_drawn_inputs(seed))
    spreads = {'L0_attn_ln_g': (1.0, 0.2),
     'L0_attn_ln_b': (0.0, 0.352),
     'L0_attn_w1_b': (0.0, 0.454),
     'L0_attn_v1_b': (0.0, 0.274),
     'L0_attn_w2_b': (0.0, 0.274),
     'L0_attn_D_skip': (1.0, 0.584),
     'L0_attn_b_dt': (-4.0, 0.6),
     'L0_ffn_q_scale': (1.0, 0.6),
     'L0_ffn_k_scale': (1.0, 0.6),
     'L0_ffn_ln_g': (1.0, 0.6),
     'L0_ffn_ln_b': (0.0, 0.8),
     'L0_ffn_b1': (0.0, 0.8),
     'L0_ffn_b2': (0.0, 0.1)}
    factors = {'L0_attn_A_log': 8.098, 'L0_attn_W_dt': 37.975, 'L0_ffn_W1': 3.208, 'L0_ffn_W2': 3.145}
    for name, (base, spread) in spreads.items():
        noise = np.random.default_rng([zlib.crc32(name.encode()), seed]).standard_normal(out[name].shape)
        drawn = base * np.exp(spread * noise) if base else spread * noise
        out[name] = jnp.asarray(drawn.astype(out[name].dtype))
    for name, factor in factors.items():
        out[name] = (out[name] * factor).astype(out[name].dtype)
    return out
```

```python
from contextlib import ExitStack

import numpy as np

import concourse.bass as bass
from concourse import mybir

F32 = mybir.dt.float32
BF16 = mybir.dt.bfloat16
ALU = mybir.AluOpType
ACT = mybir.ActivationFunctionType
AX = mybir.AxisListType

P = 128
BATCH, SEQ = 8, 256
HEADS, DH = 16, 64
PAIRS = HEADS // 2
WIN = 32
NWIN = SEQ // WIN
CHUNK_SEQS = 2
COLS = CHUNK_SEQS * SEQ
CHUNKS = BATCH // CHUNK_SEQS
TOKENS = BATCH * SEQ
DEPTH = 6
INNER = HEADS * DH
HIDDEN = int(P * 4 * 2 / 3)
HIDDEN_CUTS = [(a, min(P, HIDDEN - a)) for a in range(0, HIDDEN, P)]
STATES = 16
QK_SCALE = 8.0
EPS = 1e-5
SUBSTEPS = PAIRS
RING = 12
V_LAG = 3
GROUPS = HEADS // 4

C_IDENT, C_CENTER, C_MEAN, C_SUMSEL = 0, P, 2 * P, 3 * P
C_TABLES = C_SUMSEL + 64
C_MASK = C_TABLES + 4 * SEQ
C_SPREAD = C_MASK + NWIN * 2 * WIN
C_END = C_SPREAD + 2 * PAIRS * P
V_QS, V_QSR, V_KS, V_KSR, V_G, V_B, V_B2, V_BA, V_BG, V_END = 0, 1, 2, 3, 4, 5, 6, 7, 10, 13
M_G, M_B, M_W1B, M_V1B, M_W2B, M_D, M_BDT, M_CONV, M_ALOG, M_END = 0, 1, 2, 3, 4, 5, 6, 7, 10, 26


def norm_row(p, which):
    return 32 * (2 * (p % 2) + which) + 2 * (p // 2)


class Signal:

    def __init__(self, sem):
        self.sem, self.count = sem, 0

    def next(self, by=1):
        self.count += by
        return (self.sem, self.count)


class Queue:

    def __init__(self):
        self.ops, self.seen = [], {}

    def __call__(self, make, after=(), signal=None, by=1):
        for event in after:
            if event is None:
                continue
            sem, value = event
            if self.seen.get(sem, 0) < value:
                self.seen[sem] = value
                self.ops.append(lambda e, s=sem, v=value: e.wait_ge(s, v))
        if make is None:
            return None
        if signal is None:
            self.ops.append(make)
            return None
        event = signal.next(by)
        self.ops.append(lambda e: make(e).then_inc(signal.sem, by))
        return event

    def run(self, e):
        for op in self.ops:
            op(e)


def macaron_kernel(nc, x_in, consts_in, vec_in, mvec_in, wqkv_in, wo_in, w1_in, w2_in,
                   mw_in, wb_in, out):
    ctx = ExitStack()
    with ctx:
        def sb(name, shape, dt=F32):
            return ctx.enter_context(nc.sbuf_tensor(name, shape, dt))

        def bank(name):
            return ctx.enter_context(nc.psum_tensor(name, [P, COLS], F32))

        def sig(name):
            return Signal(ctx.enter_context(nc.semaphore(name)))

        consts = sb("consts", [P, C_END])
        ident = consts[:, C_IDENT:C_IDENT + P]
        center = consts[:, C_CENTER:C_CENTER + P]
        mean = consts[:, C_MEAN:C_MEAN + P]
        table = [consts[:, C_TABLES + i * SEQ:C_TABLES + (i + 1) * SEQ].unsqueeze(1)
                 .broadcast_to([P, CHUNK_SEQS, SEQ]) for i in range(4)]
        mask_bf = sb("mask_bf", [P, NWIN * 2 * WIN], BF16)
        ident_bf = sb("ident_bf", [P, P], BF16)
        vec = sb("vec", [P, DEPTH * V_END])
        x = sb("x", [P, TOKENS])
        xs = sb("xs", [P, BATCH, SEQ])
        wqk = sb("wqk", [P, PAIRS, 2, P])
        wrot = sb("wrot", [P, PAIRS, 2, P])
        wv = sb("wv", [P, 2, INNER])
        wo = sb("wo", [P, PAIRS, P])
        w1 = sb("w1", [P, 2 * HIDDEN])
        w2 = sb("w2", [P, len(HIDDEN_CUTS), P])
        qk_ring = [sb("q_ring", [P, RING, COLS]), sb("k_ring", [P, RING, COLS])]
        v_buf = sb("v_buf", [P, 2, 2 * NWIN, 4 * DH])
        squares = sb("squares", [P, 4, COLS])
        turned = [sb("turned_a", [P, 2, COLS]), sb("turned_b", [P, 2, COLS])]
        inv_norm = sb("inv_norm", [P, COLS])
        att = sb("att", [P, PAIRS, COLS])
        row_max = sb("row_max", [P, 2, NWIN])
        row_sum = sb("row_sum", [P, 2, NWIN])
        row_inv = sb("row_inv", [P, 2, NWIN])
        shifted = sb("shifted", [P, COLS])
        probs = sb("probs", [P, 2, COLS])
        probs_t = sb("probs_t", [P, 2, COLS])
        centered = sb("centered", [P, COLS])
        rstd = sb("rstd", [P, COLS])
        gelu_gate = sb("gelu_gate", [P, COLS])
        hidden = sb("hidden", [P, len(HIDDEN_CUTS), COLS])
        base_dram = nc.dram_tensor("base_dram", [P, TOKENS], F32).ap()

        proj, proj_rot = bank("proj"), bank("proj_rot")
        scores = bank("scores")
        attp = [bank("attp0"), bank("attp1")]
        sums = bank("sums")
        general = [bank("general0"), bank("general1")]

        pe, dve, act, pool, sp = Queue(), Queue(), Queue(), Queue(), Queue()
        by_name = {}

        def S(name):
            if name not in by_name:
                by_name[name] = sig(name)
            return by_name[name]

        def barrier():
            for q in (pe, dve, act, pool, sp):
                q(None, [(s.sem, s.count) for s in by_name.values() if s.count])

        gen_state = {"n": 0, "read": [None, None]}

        def take_bank():
            i = gen_state["n"] % 2
            gen_state["n"] += 1
            return i, general[i], gen_state["read"][i]

        def bank_read(i, event):
            gen_state["read"][i] = event

        ev_const = sp(lambda e: e.dma_start(consts[:, :], consts_in), signal=S("consts_loaded"), by=16)
        ev_vec = sp(lambda e: e.dma_start(vec[:, :], vec_in), signal=S("vec_loaded"), by=16)
        dve(lambda e: e.tensor_copy(mask_bf[:, :], consts[:, C_MASK:C_SPREAD]), [ev_const])
        ev_bf = dve(lambda e: e.tensor_copy(ident_bf[:, :], ident), signal=S("bf16_consts"))
        ev_zero = pool(lambda e: e.memset(xs[:, :, :], 0.0), signal=S("shift_zeroed"))

        staging = qk_ring[0]
        x_tiles = x_in.rearrange("b (h p) d -> p (b h) d", p=P)
        stage_v = staging[:, 0:4, :].rearrange("p r (h d) -> p (r h) d", d=P)
        ev_in = sp(lambda e: e.dma_start(stage_v, x_tiles), signal=S("x_loaded"), by=16)
        ev = None
        x_ready = [None] * CHUNKS
        for c in range(CHUNKS):
            i, g, free = take_bank()
            for j in range(4):
                ev = pe(lambda e, c=c, j=j, g=g: e.transpose(g[:, j * P:(j + 1) * P],
                        stage_v[:, 4 * c + j, :], ident), [free, ev_in, ev_const],
                        signal=S("x_turned") if j == 3 else None)
            x_ready[c] = dve(lambda e, c=c, g=g: e.tensor_copy(x[:, c * COLS:(c + 1) * COLS], g[:, :]),
                             [ev], signal=S("x_kept"))
            bank_read(i, x_ready[c])

        last = {"centered_read": None, "rstd_read": None}

        def norm_center(src, ready):
            i, g, free = take_bank()
            ev = pe(lambda e: e.matmul(g[:, :], center, src, start=True, stop=True),
                    [free, ready], signal=S("ln_centered"))
            ev = dve(lambda e: e.tensor_copy(centered[:, :], g[:, :]),
                     [ev, last["centered_read"]], signal=S("ln_center_kept"))
            bank_read(i, ev)
            return pool(lambda e: e.tensor_tensor(rstd[:, :], centered[:, :], centered[:, :], ALU.mult),
                        [ev, last["rstd_read"]], signal=S("ln_squared"))

        def norm_var(squared):
            i, g, free = take_bank()
            ev = pe(lambda e: e.matmul(g[:, :], mean, rstd[:, :], start=True, stop=True),
                    [free, squared], signal=S("ln_var"))
            ev = dve(lambda e: e.tensor_scalar(rstd[:, :], g[:, :], EPS, None, ALU.add),
                     [ev], signal=S("ln_var_kept"))
            bank_read(i, ev)
            return dve(lambda e: e.reciprocal(rstd[:, :], rstd[:, :]), [ev], signal=S("ln_inv"))

        def norm_apply(inv, dst, gain=None, bias=None, dst_free=()):
            ev = act(lambda e: e.activation(rstd[:, :], rstd[:, :], ACT.Sqrt), [inv], signal=S("ln_rstd"))
            to = dst if gain is None else centered[:, :]
            ev = pool(lambda e: e.tensor_tensor(to, centered[:, :], rstd[:, :], ALU.mult),
                      [ev, *dst_free], signal=S("ln_scaled"))
            last["rstd_read"] = last["centered_read"] = ev
            if gain is not None:
                ev = pool(lambda e: e.tensor_scalar(dst, centered[:, :], gain, bias, ALU.mult, ALU.add),
                          [ev], signal=S("ln_affine"))
                last["centered_read"] = ev
            return ev

        xs_read = [None] * CHUNKS

        def shift_tokens(c, ready, x_wait=None):
            src = x[:, c * COLS:(c + 1) * COLS].rearrange("p (s t) -> p s t", s=CHUNK_SEQS)
            dst = xs[:, c * CHUNK_SEQS:(c + 1) * CHUNK_SEQS, :]
            act(lambda e: e.activation(dst[0:64, :, :], src[0:64, :, :], ACT.Copy),
                [ready, xs_read[c], ev_zero])
            return act(lambda e: e.activation(dst[64:P, :, 1:SEQ], src[64:P, :, 0:SEQ - 1], ACT.Copy),
                       signal=S("shifted_tokens"))

        items = [(layer, c) for layer in range(DEPTH) for c in range(CHUNKS)]
        slot_free = {"wqk": [None] * PAIRS, "wrot": [None] * PAIRS, "wv": [None, None],
                     "wo": None, "w1": None, "w2": None}
        w_ready = {}
        ring_read = [[None] * RING, [None] * RING]
        v_read = [None, None]
        att_read = {"wo": None}
        misc = {"squares": [None] * 4, "turned": [[None] * 2, [None] * 2], "proj": None, "proj_rot": None,
                "scores": None, "attp": [None, None], "sums_read": None, "inv_norm_read": None,
                "shifted_read": None, "probs_read": [None, None], "probs_t_read": [None, None],
                "hidden_read": None, "gelu_read": None}
        vround = {"n": 0}

        def stack(xs_ready):
            state = {}
            x_state = list(xs_ready)

            def load_pair(layer, p):
                src = wqkv_in[layer].rearrange("d (k c) -> d k c", k=3)[:, 0:2, p * P:(p + 1) * P]
                ev = sp(lambda e: e.dma_start(wqk[:, p, :, :], src),
                        [slot_free["wqk"][p], slot_free["wrot"][p]], signal=S(f"wqk{p}_loaded"), by=16)
                a = wqk[:, p, :, :].rearrange("d k (h f c) -> d (k h) f c", h=2, f=2)
                b = wrot[:, p, :, :].rearrange("d k (h f c) -> d (k h) f c", h=2, f=2)
                pool(lambda e: e.tensor_copy(b[:, :, 0, :], a[:, :, 1, :]), [ev, slot_free["wrot"][p]])
                rot = pool(lambda e: e.tensor_copy(b[:, :, 1, :], a[:, :, 0, :]), signal=S("wrot_made"))
                w_ready["wqk", layer, p] = ev
                w_ready["wrot", layer, p] = rot

            def load_v(layer):
                i = vround["n"] % 2
                vround["n"] += 1
                w_ready["wv", layer] = (i, sp(lambda e: e.dma_start(wv[:, i, :], wqkv_in[layer][:, 2 * INNER:]),
                                              [slot_free["wv"][i]], signal=S(f"wv{i}_loaded"), by=16))

            def load_wo(layer):
                src = wo_in[layer].rearrange("(p d) n -> d p n", d=P)
                w_ready["wo", layer] = sp(lambda e: e.dma_start(wo[:, :, :], src), [slot_free["wo"]],
                                          signal=S("wo_loaded"), by=16)

            def load_w1(layer):
                w_ready["w1", layer] = sp(lambda e: e.dma_start(w1[:, :], w1_in[layer]), [slot_free["w1"]],
                                          signal=S("w1_loaded"), by=16)

            def load_w2(layer):
                full = len(HIDDEN_CUTS) - 1
                src = w2_in[layer][0:full * P, :].rearrange("(j d) n -> d j n", d=P)
                sp(lambda e: e.dma_start(w2[:, 0:full, :], src), [slot_free["w2"]],
                   signal=S("w2_loaded"), by=16)
                a, n = HIDDEN_CUTS[-1]
                w_ready["w2", layer] = sp(lambda e: e.dma_start(w2[0:n, full, :], w2_in[layer][a:a + n, :]),
                                          signal=S("w2_loaded"), by=16)

            def vcol(layer, i):
                return vec[:, layer * V_END + i:layer * V_END + i + 1]

            def project(n, p, which):
                layer, c = items[n]
                rhs = xs[:, c * CHUNK_SEQS:(c + 1) * CHUNK_SEQS, :]
                ready = x_state[c]
                pr = pe(lambda e: e.matmul(proj_rot[:, :], wrot[:, p, which, :], rhs, start=True, stop=True),
                        [ready, w_ready["wrot", layer, p], misc["proj_rot"]], signal=S("proj_rot_done"))
                pp = pe(lambda e: e.matmul(proj[:, :], wqk[:, p, which, :], rhs, start=True, stop=True),
                        [w_ready["wqk", layer, p], misc["proj"]], signal=S("proj_done"))
                slot_free["wqk"][p] = slot_free["wrot"][p] = pp
                sq = (2 * p + which) % 4
                sq_ev = act(lambda e: e.activation(squares[:, sq, :], proj[:, :], ACT.Square),
                            [pp, misc["squares"][sq]], signal=S("squared"))
                t = which
                a, b = turned[0][:, t, :], turned[1][:, t, :]
                p3 = proj[:, :].rearrange("p (s t) -> p s t", s=CHUNK_SEQS)
                r3 = proj_rot[:, :].rearrange("p (s t) -> p s t", s=CHUNK_SEQS)
                a3, b3 = (y.rearrange("p (s t) -> p s t", s=CHUNK_SEQS) for y in (a, b))
                rb = dve(lambda e: e.scalar_tensor_tensor(out=b3, in0=r3, scalar=vcol(layer, V_QSR + 2 * which),
                         in1=table[2 * which + 1], op0=ALU.mult, op1=ALU.mult),
                         [pr, misc["turned"][1][t], ev_vec, ev_const], signal=S("turned_rot"))
                ra = dve(lambda e: e.scalar_tensor_tensor(out=a3, in0=p3, scalar=vcol(layer, V_QS + 2 * which),
                         in1=table[2 * which], op0=ALU.mult, op1=ALU.mult),
                         [pp, sq_ev, misc["turned"][0][t]], signal=S("turned_plain"))
                misc["proj_rot"], misc["proj"] = rb, ra
                slot = (n * PAIRS + p) % RING
                done = pool(lambda e: e.tensor_tensor(qk_ring[which][:, slot, :], a, b, ALU.add),
                            [ra, rb, ring_read[which][slot]], signal=S("rotated"))
                misc["turned"][0][t] = misc["turned"][1][t] = done
                state[n]["sq", p, which] = sq_ev
                state[n]["rot", p, which] = done

            def sum_squares(n, couple):
                for j in range(4):
                    p, which = 2 * couple + j // 2, j % 2
                    sel = consts[:, C_SUMSEL + 30 - 2 * couple:C_SUMSEL + 62 - 2 * couple]
                    wait = [state[n]["sq", p, which]]
                    if couple == 0:
                        wait += [misc["sums_read"], ev_const]
                    ev = pe(lambda e, j=j, sel=sel: e.matmul(sums[32 * j:32 * j + 32, :], sel,
                            squares[:, j, :], start=(couple == 0), stop=(couple == PAIRS // 2 - 1)),
                            wait, signal=S("squares_summed") if j == 3 else None)
                misc["squares"] = [ev] * 4
                state[n]["sums"] = ev

            def invert_norms(n):
                ev = dve(lambda e: e.tensor_scalar(inv_norm[:, :], sums[:, :], 1e-24, None, ALU.max),
                         [state[n]["sums"], misc["inv_norm_read"]], signal=S("sums_kept"))
                misc["sums_read"] = ev
                ev = dve(lambda e: e.reciprocal(inv_norm[:, :], inv_norm[:, :]), [ev], signal=S("sums_inverted"))
                state[n]["inv"] = act(lambda e: e.activation(inv_norm[:, :], inv_norm[:, :], ACT.Sqrt),
                                      [ev], signal=S("norms_inverted"))

            def project_v(n, p):
                layer, c = items[n]
                i, g, free = take_bank()
                wi, wv_ready = w_ready["wv", layer]
                for w in range(2):
                    win = 2 * p + w
                    lhs = xs[:, c * CHUNK_SEQS + win // NWIN, (win % NWIN) * WIN:(win % NWIN + 1) * WIN]
                    for q in range(4):
                        rhs = wv[:, wi, :].rearrange("d (r g c) -> d g r c", g=4, c=DH)[:, q, :, :]
                        o = g[32 * q:32 * q + 32, w * 256:(w + 1) * 256]
                        ev = pe(lambda e, o=o, lhs=lhs, rhs=rhs: e.matmul(o, lhs, rhs, start=True, stop=True),
                                [free, wv_ready, x_state[c]],
                                signal=S("v_projected") if w == 1 and q == 3 else None)
                slot_free["wv"][wi] = ev
                xs_read[c] = ev
                to = v_buf[:, n % 2, 2 * p:2 * p + 2, :]
                ev = act(lambda e: e.activation(to, g[:, :].rearrange("p (w c) -> p w c", w=2), ACT.Copy),
                         [ev, v_read[n % 2]], signal=S("v_kept"))
                bank_read(i, ev)
                state[n]["v"] = ev

            def normalise(n, p, which):
                i, g, free = take_bank()
                at = C_SPREAD + (2 * p + which) * P
                sel = consts[:, at:at + P]
                ev = pe(lambda e: e.matmul(g[:, :], sel, inv_norm[:, :], start=True, stop=True),
                        [free, state[n]["inv"]], signal=S("norm_spread"))
                misc["inv_norm_read"] = ev
                slot = (n * PAIRS + p) % RING
                y = qk_ring[which][:, slot, :]
                ev = dve(lambda e: e.tensor_tensor(y, y, g[:, :], ALU.mult),
                         [ev, state[n]["rot", p, which]], signal=S("normalised"))
                bank_read(i, ev)
                state[n]["norm", p, which] = ev

            def attend_scores(n, s):
                group, seq = s // CHUNK_SEQS, s % CHUNK_SEQS
                pe(lambda e: e.matmul(scores[:, :], ident_bf[:, :], mask_bf[:, :], start=True, stop=False,
                                      skip_group_check=True),
                   [misc["scores"], ev_bf] + [state[n]["norm", 2 * group + j, k] for j in range(2) for k in range(2)])
                for w in range(NWIN):
                    for h in range(4):
                        slot = (n * PAIRS + 2 * group + h // 2) % RING
                        r0 = DH * (h % 2)
                        t0 = seq * SEQ + w * WIN
                        back = WIN if w else 0
                        qw = qk_ring[0][r0:r0 + DH, slot, t0:t0 + WIN]
                        kw = qk_ring[1][r0:r0 + DH, slot, t0 - back:t0 + WIN]
                        o = scores[32 * h:32 * h + 32, w * 2 * WIN + WIN - back:(w + 1) * 2 * WIN]
                        end = w == NWIN - 1 and h == 3
                        ev = pe(lambda e, o=o, qw=qw, kw=kw: e.matmul(o, qw, kw, start=False, stop=True,
                                skip_group_check=True), signal=S("scored") if end else None)
                for j in range(2):
                    slot = (n * PAIRS + 2 * group + j) % RING
                    ring_read[0][slot] = ring_read[1][slot] = ev
                b = s % 2
                s3 = scores[:, :].rearrange("p (w k) -> p w k", w=NWIN)

                def spread(y):
                    return y[:, b, :].unsqueeze(2).broadcast_to([P, NWIN, 2 * WIN])

                def cube(y):
                    return y.rearrange("p (w k) -> p w k", w=NWIN)

                ev = dve(lambda e: e.tensor_reduce(row_max[:, b, :], s3, AX.X, ALU.max), [ev], signal=S("row_max"))
                ev = dve(lambda e: e.tensor_tensor(cube(shifted[:, :]), s3, spread(row_max), ALU.subtract),
                         [ev, misc["shifted_read"]], signal=S("max_off"))
                misc["scores"] = ev
                ev = act(lambda e: e.activation(probs[:, b, :], shifted[:, :], ACT.Exp, scale=QK_SCALE),
                         [ev, misc["probs_read"][b]], signal=S("exponent"))
                misc["shifted_read"] = ev
                state[n]["exp", s] = ev

            def attend_probs(n, s):
                b = s % 2

                def spread(y):
                    return y[:, b, :].unsqueeze(2).broadcast_to([P, NWIN, 2 * WIN])

                def cube(y):
                    return y.rearrange("p (w k) -> p w k", w=NWIN)

                ev = dve(lambda e: e.tensor_reduce(row_sum[:, b, :], cube(probs[:, b, :]), AX.X, ALU.add),
                         [state[n]["exp", s]], signal=S("row_sum"))
                ev = dve(lambda e: e.reciprocal(row_inv[:, b, :], row_sum[:, b, :]), [ev], signal=S("row_inv"))
                ev = pool(lambda e: e.tensor_tensor(cube(probs[:, b, :]), cube(probs[:, b, :]), spread(row_inv),
                                                    ALU.mult), [ev], signal=S("probs_done"))
                ev = dve(lambda e: e.transpose(probs_t[:, b, :], probs[:, b, :]),
                         [ev, misc["probs_t_read"][b]], signal=S("probs_turned"))
                misc["probs_read"][b] = ev
                state[n]["pt", s] = ev

            def attend_values(n, s):
                group, seq = s // CHUNK_SEQS, s % CHUNK_SEQS
                b = s % 2
                for kb in range(NWIN):
                    width = 2 * WIN if kb < NWIN - 1 else WIN
                    for h in range(4):
                        lhs = v_buf[32 * h:32 * h + 32, n % 2, seq * NWIN + kb, group * DH:(group + 1) * DH]
                        rhs = probs_t[32 * h:32 * h + 32, b, kb * 64 + WIN:kb * 64 + WIN + width]
                        o = attp[h // 2][DH * (h % 2):DH * (h % 2) + DH, kb * WIN:kb * WIN + width]
                        end = kb == NWIN - 1 and h == 3
                        ev = pe(lambda e, o=o, lhs=lhs, rhs=rhs, kb=kb: e.matmul(o, lhs, rhs, start=(kb == 0),
                                stop=True, skip_group_check=True),
                                [state[n]["pt", s], state[n]["v"], *misc["attp"]],
                                signal=S("valued") if end else None)
                misc["probs_t_read"][b] = ev
                v_read[n % 2] = ev
                for j in range(2):
                    to = att[:, 2 * group + j, seq * SEQ:(seq + 1) * SEQ]
                    k = act(lambda e, j=j, to=to: e.activation(to, attp[j][:, 0:SEQ], ACT.Copy),
                            [ev, att_read["wo"]], signal=S("att_kept"))
                    misc["attp"][j] = k
                state[n]["att"] = k

            def project_out(n):
                layer, c = items[n]
                i, g, free = take_bank()
                for p in range(PAIRS):
                    ev = pe(lambda e, p=p: e.matmul(g[:, :], wo[:, p, :], att[:, p, :], start=(p == 0),
                                                    stop=(p == PAIRS - 1)),
                            [free, w_ready["wo", layer], state[n]["att"]],
                            signal=S("out_projected") if p == PAIRS - 1 else None)
                att_read["wo"] = slot_free["wo"] = ev
                xc = x[:, c * COLS:(c + 1) * COLS]
                ev = dve(lambda e: e.tensor_tensor(xc, xc, g[:, :], ALU.add), [ev, x_state[c]],
                         signal=S("att_added"))
                bank_read(i, ev)
                x_state[c] = shift_tokens(c, ev)
                if c == CHUNKS - 1 and layer + 1 < DEPTH:
                    load_wo(layer + 1)

            def ffn_center(n):
                c = items[n][1]
                rhs = xs[:, c * CHUNK_SEQS:(c + 1) * CHUNK_SEQS, :]
                state[n]["lnsq"] = norm_center(rhs, x_state[c])
                xs_read[c] = (S("ln_centered").sem, S("ln_centered").count)

            def ffn_var(n):
                state[n]["lninv"] = norm_var(state[n]["lnsq"])

            def ffn_norm(n):
                layer = items[n][0]
                state[n]["xn"] = norm_apply(state[n]["lninv"], centered[:, :], vcol(layer, V_G), vcol(layer, V_B))

            def ffn_hidden(n):
                layer = items[n][0]
                for j, (a, m) in enumerate(HIDDEN_CUTS):
                    i, g, free = take_bank()
                    ev = pe(lambda e, g=g, a=a, m=m: e.matmul(g[0:m, :], w1[:, HIDDEN + a:HIDDEN + a + m],
                            centered[:, :], start=True, stop=True),
                            [free, w_ready["w1", layer], state[n]["xn"]], signal=S("gate_done"))
                    gate = act(lambda e, g=g, m=m, j=j: e.activation(gelu_gate[0:m, :], g[0:m, :], ACT.Gelu,
                               bias=vcol(layer, V_BG + j)[0:m, :]), [ev, misc["gelu_read"]], signal=S("gelu_done"))
                    bank_read(i, gate)
                    i, g, free = take_bank()
                    ev = pe(lambda e, g=g, a=a, m=m: e.matmul(g[0:m, :], w1[:, a:a + m], centered[:, :],
                                                              start=True, stop=True), [free], signal=S("value_done"))
                    ev2 = dve(lambda e, g=g, m=m, j=j: e.scalar_tensor_tensor(out=hidden[0:m, j, :], in0=g[0:m, :],
                              scalar=vcol(layer, V_BA + j)[0:m, :], in1=gelu_gate[0:m, :], op0=ALU.add,
                              op1=ALU.mult), [ev, gate, misc["hidden_read"]], signal=S("hidden_done"))
                    misc["gelu_read"] = ev2
                    bank_read(i, ev2)
                last["centered_read"] = slot_free["w1"] = ev
                state[n]["hidden"] = ev2
                if items[n][1] == CHUNKS - 1 and layer + 1 < DEPTH:
                    load_w1(layer + 1)

            def ffn_out(n):
                layer, c = items[n]
                i, g, free = take_bank()
                for j, (a, m) in enumerate(HIDDEN_CUTS):
                    ev = pe(lambda e, j=j, m=m: e.matmul(g[:, :], w2[0:m, j, :], hidden[0:m, j, :],
                            start=(j == 0), stop=(j == len(HIDDEN_CUTS) - 1)),
                            [free, w_ready["w2", layer], state[n]["hidden"]],
                            signal=S("ffn_done") if j == len(HIDDEN_CUTS) - 1 else None)
                misc["hidden_read"] = slot_free["w2"] = ev
                xc = x[:, c * COLS:(c + 1) * COLS]
                ev = dve(lambda e: e.scalar_tensor_tensor(out=xc, in0=g[:, :], scalar=vcol(layer, V_B2), in1=xc,
                         op0=ALU.add, op1=ALU.add), [ev, x_state[c]], signal=S("ffn_added"))
                bank_read(i, ev)
                x_state[c] = shift_tokens(c, ev)
                if c == CHUNKS - 1 and layer + 1 < DEPTH:
                    load_w2(layer + 1)

            load_v(0)
            for p in range(PAIRS):
                load_pair(0, p)
            load_wo(0)
            load_w1(0)
            load_w2(0)
            N = len(items)
            C_STEPS = {3: project_out, 4: ffn_center, 6: ffn_var, 8: ffn_norm, 9: ffn_hidden, 10: ffn_out}
            for t in range(SUBSTEPS * (N + 3) + 3):
                for k, stage in C_STEPS.items():
                    n = (t - k) // SUBSTEPS - 2
                    if (t - k) % SUBSTEPS == 0 and 0 <= n < N:
                        stage(n)
                n, p = divmod(t, SUBSTEPS)
                if p % 2 == 0:
                    m, couple = (n, p // 2 - 1) if p else (n - 1, PAIRS // 2 - 1)
                    if 0 <= m < N and couple >= 0:
                        sum_squares(m, couple)
                        if p == 0:
                            invert_norms(m)
                bn, bs = divmod(t - SUBSTEPS - 2, SUBSTEPS)
                cn, cs = divmod(t - SUBSTEPS - 3, SUBSTEPS)
                if 0 <= n < N:
                    if p == 0:
                        state[n] = {}
                    project(n, p, 0)
                if 0 <= cn < N:
                    attend_probs(cn, cs)
                if 0 <= bn < N:
                    attend_scores(bn, bs)
                if 0 <= n < N:
                    project(n, p, 1)
                if 0 <= cn < N:
                    attend_values(cn, cs)
                vn, vp = divmod(t - V_LAG, SUBSTEPS)
                if 0 <= vn < N:
                    project_v(vn, vp)
                if 0 <= n < N:
                    layer, c = items[n]
                    if c == CHUNKS - 1 and layer + 1 < DEPTH:
                        load_pair(layer + 1, p)
                        if p == 0:
                            load_v(layer + 1)
                if 0 <= n - 1 < N:
                    normalise(n - 1, p, 0)
                    normalise(n - 1, p, 1)
            return x_state

        def layer_norm(c, ready, dst, gain=None, bias=None):
            sq = norm_center(x[:, c * COLS:(c + 1) * COLS], ready)
            return norm_apply(norm_var(sq), dst, gain, bias)

        def half_step(ready, load_first):
            stored = [sp(lambda e, c=c: e.dma_start(base_dram[:, c * COLS:(c + 1) * COLS],
                      x[:, c * COLS:(c + 1) * COLS]), [ready[c]], signal=S("base_stored"), by=16)
                      for c in range(CHUNKS)]
            xs_ready = []
            for c in range(CHUNKS):
                ev = layer_norm(c, ready[c], x[:, c * COLS:(c + 1) * COLS]) if False else None
                sq = norm_center(x[:, c * COLS:(c + 1) * COLS], ready[c])
                ev = norm_apply(norm_var(sq), x[:, c * COLS:(c + 1) * COLS], dst_free=[stored[-1]])
                xs_ready.append(shift_tokens(c, ev))
            ends = stack(xs_ready)
            done = []
            for c in range(CHUNKS):
                base = qk_ring[0][:, c, :]
                ev = sp(lambda e, c=c, base=base: e.dma_start(base, base_dram[:, c * COLS:(c + 1) * COLS]),
                        [stored[-1], *ring_read[0]], signal=S(f"base{c}_loaded"), by=16)
                xc = x[:, c * COLS:(c + 1) * COLS]
                done.append(dve(lambda e, xc=xc, base=base: e.scalar_tensor_tensor(out=xc, in0=xc, scalar=0.5,
                            in1=base, op0=ALU.mult, op1=ALU.add), [ev, ends[c]], signal=S("half_added")))
                for w in (0, 1):
                    ring_read[w] = [done[-1]] * RING
            return done

        def scan_block():
            barrier()
            pool_a = [qk_ring[0][:, i, :] for i in range(RING)]
            pool_b = [qk_ring[1][:, i, :] for i in range(RING)]
            xn, u, z, dt, dtu, acc, e1, ln1, gate, corr = pool_a[:10]
            decay = [pool_b[0], pool_b[1]]
            drive = [pool_b[2], pool_b[3]]
            hstate = [pool_b[4], pool_b[5]]
            hc = [pool_b[6], pool_b[7]]
            padded = v_buf[:, 0, 0:3, :].rearrange("p w c -> p (w c)")[:, 0:CHUNK_SEQS * (SEQ + 2)]\
                .rearrange("p (s t) -> p s t", s=CHUNK_SEQS)
            mw = v_buf[:, 1, 0:2, :].rearrange("p w c -> p (w c)")[:, 0:4 * P].rearrange("p (m n) -> p m n", m=4)
            wbc = v_buf[:, 1, 2, 0:2 * STATES]
            mvec = v_buf[:, 1, 3, 0:M_END]
            neg_a = v_buf[:, 1, 4, 0:STATES]

            def mcol(i):
                return mvec[:, i:i + 1]

            sp(lambda e: e.dma_start(mw, mw_in.rearrange("m d n -> d m n")), signal=S("m_loaded"), by=16)
            sp(lambda e: e.dma_start(wbc, wb_in), signal=S("m_loaded"), by=16)
            ev_m = sp(lambda e: e.dma_start(mvec, mvec_in), signal=S("m_loaded"), by=16)
            act(lambda e: e.activation(neg_a, mvec[:, M_ALOG:M_ALOG + STATES], ACT.Exp), [ev_m],
                signal=S("m_a"))
            ev_a = act(lambda e: e.mul(neg_a, neg_a, -1.0), [(S("m_a").sem, S("m_a").count)], signal=S("m_a"))
            ev_pad = pool(lambda e: e.memset(padded, 0.0), signal=S("m_pad"))
            acc_read = dtu_read = None
            rd = {"drive": [None, None], "hc": [None, None], "h": [None, None], "decay": [None, None]}
            done = []
            chain = S("m_dve")

            def D(make, after=()):
                return dve(make, [*after, (chain.sem, chain.count)] if chain.count else after, signal=chain)

            for c in range(CHUNKS):
                xc = x[:, c * COLS:(c + 1) * COLS]
                prev = done[-1] if done else None
                ev = layer_norm(c, prev, xn)
                sq = norm_center(xn, ev)
                ev = norm_apply(norm_var(sq), xn, mcol(M_G), mcol(M_B))

                def linear(m, rhs, ready):
                    i, g, free = take_bank()
                    return i, g, pe(lambda e: e.matmul(g[:, :], mw[:, m, :], rhs, start=True, stop=True),
                                    [free, ready, ev_m], signal=S("m_linear"))

                ev_xn = ev
                i, g, ev = linear(0, xn, ev_xn)
                g3 = g[:, :].rearrange("p (s t) -> p s t", s=CHUNK_SEQS)
                ev = D(lambda e, g3=g3: e.tensor_scalar(padded[:, :, 1:SEQ + 1], g3, mcol(M_W1B), None, ALU.add),
                       [ev, ev_pad])
                bank_read(i, ev)
                u3 = u.rearrange("p (s t) -> p s t", s=CHUNK_SEQS)
                D(lambda e: e.tensor_scalar(u3, padded[:, :, 0:SEQ], mcol(M_CONV), None, ALU.mult), [ev_m])
                D(lambda e: e.scalar_tensor_tensor(out=u3, in0=padded[:, :, 1:SEQ + 1], scalar=mcol(M_CONV + 1),
                  in1=u3, op0=ALU.mult, op1=ALU.add))
                ev = D(lambda e: e.scalar_tensor_tensor(out=u3, in0=padded[:, :, 2:SEQ + 2], scalar=mcol(M_CONV + 2),
                       in1=u3, op0=ALU.mult, op1=ALU.add))
                ev_u = act(lambda e: e.activation(u, u, ACT.Silu), [ev], signal=S("m_u"))
                i, g, ev = linear(1, xn, ev_xn)
                ev_gate = act(lambda e, g=g: e.activation(gate, g[:, :], ACT.Silu, bias=mcol(M_V1B)), [ev],
                              signal=S("m_gate"))
                bank_read(i, ev_gate)
                i, g, ev = linear(2, u, ev_u)
                ev = D(lambda e, g=g: e.tensor_scalar(z, g[:, :], mcol(M_BDT), None, ALU.add), [ev])
                bank_read(i, ev)
                ev = D(lambda e: e.scalar_tensor_tensor(out=e1, in0=z, scalar=-1.0, in1=z, op0=ALU.mult, op1=ALU.min))
                ev = act(lambda e: e.activation(e1, e1, ACT.Exp), [ev], signal=S("m_exp"))
                ev_w = D(lambda e: e.tensor_scalar(corr, e1, 1.0, None, ALU.add), [ev])
                ev_l = act(lambda e: e.activation(ln1, corr, ACT.Ln), [ev_w], signal=S("m_ln"))
                D(lambda e: e.scalar_tensor_tensor(out=corr, in0=corr, scalar=1.0, in1=e1, op0=ALU.subtract,
                  op1=ALU.subtract), [ev_l])
                D(lambda e: e.tensor_tensor(ln1, ln1, corr, ALU.subtract))
                ev_dt = D(lambda e: e.scalar_tensor_tensor(out=dt, in0=z, scalar=0.0, in1=ln1, op0=ALU.max,
                          op1=ALU.add))
                ev_dtu = D(lambda e: e.tensor_tensor(dtu, dt, u, ALU.mult), [ev_u])
                ev_acc = pool(lambda e: e.tensor_scalar(acc, u, mcol(M_D), None, ALU.mult), [ev_u, acc_read],
                              signal=S("m_acc"))
                for s in range(STATES):
                    b = s % 2
                    ev_dec = act(lambda e, s=s, b=b: e.activation(decay[b], dt, ACT.Exp, scale=neg_a[:, s:s + 1]),
                                 [ev_dt, ev_a, rd["decay"][b]], signal=S("m_decay"))
                    i, g, free = take_bank()
                    ev = pe(lambda e, s=s, g=g: e.matmul(g[:, :], wbc[:, s:s + 1].broadcast_to([P, P]), u,
                            start=True, stop=True), [free, ev_u, ev_m], signal=S("m_b"))
                    ev = dve(lambda e, b=b, g=g: e.tensor_tensor(drive[b], dtu, g[:, :], ALU.mult),
                             [ev, ev_dtu, rd["drive"][b]], signal=S("m_drive"))
                    bank_read(i, ev)
                    for q in range(CHUNK_SEQS):
                        cut = slice(q * SEQ, (q + 1) * SEQ)
                        ev_h = dve(lambda e, b=b, cut=cut: e.tensor_tensor_scan(hstate[b][:, cut], decay[b][:, cut],
                                   drive[b][:, cut], 0.0, ALU.mult, ALU.add), [ev, ev_dec, rd["h"][b]],
                                   signal=S("m_scan"))
                    rd["decay"][b] = rd["drive"][b] = ev_h
                    i, g, free = take_bank()
                    ev = pe(lambda e, s=s, g=g: e.matmul(g[:, :], wbc[:, STATES + s:STATES + s + 1].broadcast_to([P, P]),
                            u, start=True, stop=True), [free], signal=S("m_c"))
                    ev = dve(lambda e, b=b, g=g: e.tensor_tensor(hc[b], hstate[b], g[:, :], ALU.mult),
                             [ev, ev_h, rd["hc"][b]], signal=S("m_hc"))
                    rd["h"][b] = ev
                    bank_read(i, ev)
                    ev_acc = pool(lambda e, b=b: e.tensor_tensor(acc, acc, hc[b], ALU.add), [ev, ev_acc],
                                  signal=S("m_acc"))
                    rd["hc"][b] = ev_acc
                ev = D(lambda e: e.tensor_tensor(acc, acc, gate, ALU.mult), [ev_acc, ev_gate])
                i, g, ev = linear(3, acc, ev)
                acc_read = ev
                ev = D(lambda e, g=g, xc=xc: e.scalar_tensor_tensor(out=xc, in0=g[:, :], scalar=mcol(M_W2B), in1=xc,
                       op0=ALU.add, op1=ALU.add), [ev])
                bank_read(i, ev)
                done.append(ev)
            barrier()
            return done

        ready = half_step(x_ready, True)
        ready = scan_block()
        ready = half_step(ready, False)

        barrier()
        out_tiles = out.rearrange("b (h p) d -> p (b h) d", p=P)
        stage_out = qk_ring[1][:, 0:4, :].rearrange("p r (h d) -> p (r h) d", d=P)
        for c in range(CHUNKS):
            i, g, free = take_bank()
            for j in range(4):
                ev = pe(lambda e, c=c, j=j, g=g: e.transpose(g[:, j * P:(j + 1) * P],
                        x[:, (4 * c + j) * P:(4 * c + j + 1) * P], ident), [free, ready[c]],
                        signal=S("out_turned") if j == 3 else None)
            ev = dve(lambda e, c=c, g=g: e.tensor_copy(stage_out[:, 4 * c:4 * c + 4, :],
                     g[:, :].rearrange("p (h d) -> p h d", d=P)), [ev], signal=S("out_kept"))
            bank_read(i, ev)
            ev_out = sp(lambda e, c=c: e.dma_start(out_tiles[:, 4 * c:4 * c + 4, :], stage_out[:, 4 * c:4 * c + 4, :]),
                        [ev], signal=S("out_stored"), by=16)
        sp(None, [ev_out])

        block = ctx.enter_context(nc.Block())

        @block.sync
        def _(e):
            sp.run(e)

        @block.tensor
        def _(e):
            pe.run(e)

        @block.vector
        def _(e):
            dve.run(e)

        @block.scalar
        def _(e):
            act.run(e)

        @block.gpsimd
        def _(e):
            pool.run(e)


def constants():
    f = np.float32
    c = np.zeros((P, C_END), f)
    c[:, C_IDENT:C_IDENT + P] = np.eye(P, dtype=f)
    c[:, C_CENTER:C_CENTER + P] = np.eye(P, dtype=f) - f(1 / P)
    c[:, C_MEAN:C_MEAN + P] = f(1 / P)
    c[np.arange(P), C_SUMSEL + 30 + np.arange(P) // DH] = 1
    half = np.arange(0, DH, 2, dtype=f)
    inv_freq = (f(1) / f(10000) ** (half / f(DH))).astype(f)
    t = np.arange(SEQ, dtype=f)
    freqs = t[:, None] * inv_freq[None, :]
    freqs = np.concatenate([freqs, freqs], -1)
    base = ((half + f(0.4 * DH)) / f(1.4 * DH)).astype(f)
    power = ((t - SEQ // 2) / f(WIN // 2)).astype(f)
    scale = base[None, :] ** power[:, None]
    scale = np.concatenate([scale, scale], -1).astype(f)
    inv = (f(1) / scale).astype(f)
    sign = np.where(np.arange(DH) < DH // 2, f(-1), f(1))
    tables = [np.cos(freqs) * scale, np.sin(freqs) * scale * sign, np.cos(freqs) * inv, np.sin(freqs) * inv * sign]
    for i, y in enumerate(tables):
        c[:, C_TABLES + i * SEQ:C_TABLES + (i + 1) * SEQ] = np.tile(y.T.astype(f), (2, 1))
    i = np.arange(P)[:, None, None] % WIN
    w = np.arange(NWIN)[None, :, None]
    j = np.arange(2 * WIN)[None, None, :]
    seen = np.where(j < WIN, (j >= i) & (w > 0), j - WIN <= i)
    c[:, C_MASK:C_SPREAD] = np.where(seen, f(0), f(-1e30)).reshape(P, -1)
    for p in range(PAIRS):
        for which in range(2):
            row, at = norm_row(p, which), C_SPREAD + (2 * p + which) * P
            c[row, at:at + DH] = c[row + 1, at + DH:at + P] = 1
    return c


def kernel(**inputs):
    import concourse.bacc as bacc
    from concourse.bass_utils import run_bass_kernel_spmd

    a = {k: np.ascontiguousarray(v) for k, v in inputs.items()}
    vec = np.zeros((P, DEPTH, V_END), np.float32)
    for at, name in ((V_QS, "q_scale"), (V_KS, "k_scale")):
        s = a["L0_ffn_" + name]
        swapped = np.concatenate([s[:, DH // 2:], s[:, :DH // 2]], 1)
        vec[:, :, at] = np.concatenate([s, s], 1).T
        vec[:, :, at + 1] = np.concatenate([swapped, swapped], 1).T
    vec[:, :, V_G], vec[:, :, V_B], vec[:, :, V_B2] = a["L0_ffn_ln_g"].T, a["L0_ffn_ln_b"].T, a["L0_ffn_b2"].T
    for j, (s, n) in enumerate(HIDDEN_CUTS):
        vec[:n, :, V_BA + j] = a["L0_ffn_b1"][:, s:s + n].T
        vec[:n, :, V_BG + j] = a["L0_ffn_b1"][:, HIDDEN + s:HIDDEN + s + n].T
    m = "L0_attn_"
    mvec = np.concatenate([np.stack([a[m + k] for k in ("ln_g", "ln_b", "w1_b", "v1_b", "w2_b", "D_skip", "b_dt")], 1),
                           a[m + "conv_w"][:, 0, :], a[m + "A_log"]], 1)
    arrays = {
        "x": a[m + "x"], "consts": constants(), "vec": vec.reshape(P, -1), "mvec": np.ascontiguousarray(mvec),
        "wqkv": a["L0_ffn_Wqkv"], "wo": a["L0_ffn_Wo"], "w1": a["L0_ffn_W1"], "w2": a["L0_ffn_W2"],
        "mw": np.stack([a[m + k] for k in ("w1_w", "v1_w", "W_dt", "w2_w")]),
        "wb": np.ascontiguousarray(np.concatenate([a[m + "W_B"], a[m + "W_C"]], 1)),
    }
    nc = bacc.Bacc("TRN2", target_bir_lowering=False, num_devices=1)
    args = [nc.dram_tensor(f"in_{k}", v.shape, mybir.dt.from_np(v.dtype), kind="ExternalInput").ap() for k, v in arrays.items()]
    out = nc.dram_tensor("out", a[m + "x"].shape, F32, kind="ExternalOutput").ap()
    macaron_kernel(nc, *args, out)
    r = run_bass_kernel_spmd(nc, [{f"in_{k}": v for k, v in arrays.items()}], core_ids=[0])
    return r.results[0]["out"]
```

```python
from contextlib import ExitStack

import numpy as np

import concourse.bass as bass
from concourse import mybir

F32 = mybir.dt.float32
BF16 = mybir.dt.bfloat16
F32R = mybir.dt.float32r
ALU = mybir.AluOpType
ACT = mybir.ActivationFunctionType
AX = mybir.AxisListType

P = 128
BATCH, SEQ = 8, 256
HEADS, DH = 16, 64
PAIRS = HEADS // 2
WIN = 32
NWIN = SEQ // WIN
CHUNK_SEQS = 2
COLS = CHUNK_SEQS * SEQ
CHUNKS = BATCH // CHUNK_SEQS
TOKENS = BATCH * SEQ
DEPTH = 6
INNER = HEADS * DH
HIDDEN = int(P * 4 * 2 / 3)
HIDDEN_CUTS = [(a, min(P, HIDDEN - a)) for a in range(0, HIDDEN, P)]
STATES = 16
QK_SCALE = 8.0
EPS = 1e-5
SUBSTEPS = PAIRS
RING = 12
SCORES_LAG = SUBSTEPS + 2
PROBS_LAG = SCORES_LAG + 1
VALUES_LAG = SCORES_LAG + 2
V_LAG = 5
GROUPS = HEADS // 4
ITEM_WINS = CHUNK_SEQS * NWIN
NORM_ROWS = 2 * GROUPS

C_IDENT, C_CENTER, C_MEAN, C_SUMSEL = 0, P, 2 * P, 2 * P + 1
C_TABLES = C_SUMSEL + 64
C_STAY = C_TABLES + 4 * SEQ
C_MASK = C_STAY
C_SPREAD = C_MASK + NWIN * 2 * WIN
C_END = C_SPREAD + GROUPS * P
HEAD_ORDER = [32 * f + 16 * q + r for q in range(2) for f in range(2) for r in range(16)]
PARTNER = [(i + 16) % 32 for i in range(32)]
V_QS, V_QSR, V_KS, V_KSR, V_G, V_B, V_B2, V_BA, V_BG, V_END = 0, 1, 2, 3, 4, 5, 6, 7, 10, 13
M_G, M_B, M_W1B, M_V1B, M_W2B, M_D, M_BDT, M_CONV, M_ALOG, M_END = 0, 1, 2, 3, 4, 5, 6, 7, 10, 26


def norm_row(p, which):
    return 32 * (2 * (p % 2) + which) + 2 * (p // 2)


class Signal:

    def __init__(self, sem):
        self.sem, self.count = sem, 0

    def next(self, by=1):
        self.count += by
        return (self.sem, self.count)


class Queue:

    def __init__(self):
        self.ops, self.seen = [], {}

    def __call__(self, make, after=(), signal=None, by=1):
        for event in after:
            if event is None:
                continue
            sem, value = event
            if self.seen.get(sem, 0) < value:
                self.seen[sem] = value
                self.ops.append(lambda e, s=sem, v=value: e.wait_ge(s, v))
        if make is None:
            return None
        if signal is None:
            self.ops.append(make)
            return None
        event = signal.next(by)
        self.ops.append(lambda e: make(e).then_inc(signal.sem, by))
        return event

    def run(self, e):
        for op in self.ops:
            op(e)


def macaron_kernel(nc, x_in, consts_in, vec_in, mvec_in, wqkv_in, wo_in, w1_in, w2_in,
                   mw_in, wb_in, out):
    ctx = ExitStack()
    with ctx:
        def sb(name, shape, dt=F32):
            return ctx.enter_context(nc.sbuf_tensor(name, shape, dt))

        def bank(name):
            return ctx.enter_context(nc.psum_tensor(name, [P, COLS], F32))

        def sig(name):
            return Signal(ctx.enter_context(nc.semaphore(name)))

        consts = sb("consts", [P, C_STAY])
        ident = consts[:, C_IDENT:C_IDENT + P]
        center = consts[:, C_CENTER:C_CENTER + P]
        mean = consts[:, C_MEAN:C_MEAN + 1].broadcast_to([P, P])
        tables = consts[:, C_TABLES:C_TABLES + 4 * SEQ].rearrange("p (i t) -> p i t", i=4)
        sin_scaled = sb("sin_scaled", [P, 2, SEQ])
        mask_bf = sb("mask_bf", [P, NWIN * 2 * WIN], BF16)
        ident_bf = sb("ident_bf", [P, P], BF16)
        vec = sb("vec", [P, DEPTH * V_END])
        x = sb("x", [P, TOKENS])
        xs = sb("xs", [P, BATCH, SEQ])
        wqk_raw = sb("wqk_raw", [P, 2, 2 * P])
        wqk_hi = sb("wqk_hi", [P, PAIRS, 2 * P], F32R)
        wqk_lo = sb("wqk_lo", [P, PAIRS, 2 * P], F32R)
        xs_hi = sb("xs_hi", [P, 2, COLS], F32R)
        xs_lo = sb("xs_lo", [P, 2, COLS], F32R)
        spread_sel = sb("spread_sel", [P, GROUPS * P], F32R)
        wv = sb("wv", [P, 2, INNER])
        wo = sb("wo", [P, PAIRS, P])
        w1 = sb("w1", [P, 2 * HIDDEN])
        w2 = sb("w2", [P, len(HIDDEN_CUTS), P])
        qk_ring = [sb("q_ring", [P, RING, COLS]), sb("k_ring", [P, RING, COLS])]
        v_buf = sb("v_buf", [P, 2, 2 * NWIN, 4 * DH])
        squares = sb("squares", [P, 4, COLS])
        partner = sb("partner", [P, 2, COLS])
        inv_norm = sb("inv_norm", [P, COLS])
        norm_t = sb("norm_t", [P, ITEM_WINS, WIN])
        q_scale8 = sb("q_scale8", [P, 2, GROUPS, ITEM_WINS])
        k_inv = sb("k_inv", [P, WIN + COLS])
        inv_hi, inv_lo = sb("inv_hi", [P, COLS], F32R), sb("inv_lo", [P, COLS], F32R)
        att = sb("att", [P, PAIRS, COLS])
        row_max = sb("row_max", [P, 2, NWIN])
        row_sum = sb("row_sum", [P, 2, NWIN])
        probs = sb("probs", [P, 2, COLS])
        probs_t = sb("probs_t", [P, 2, COLS])
        centered = sb("centered", [P, COLS])
        rstd = sb("rstd", [P, COLS])
        var_t = sb("var_t", [P, ITEM_WINS, WIN])
        hidden = sb("hidden", [P, len(HIDDEN_CUTS), COLS])
        base_dram = nc.dram_tensor("base_dram", [P, TOKENS], F32).ap()

        proj = [bank("proj_q"), bank("proj_k")]
        scores = bank("scores")
        attp = [bank("attp0"), bank("attp1")]
        sums = bank("sums")
        general = [bank("general0"), bank("general1")]

        pe, dve, act, pool, sp = Queue(), Queue(), Queue(), Queue(), Queue()
        by_name = {}

        def S(name):
            if name not in by_name:
                by_name[name] = sig(name)
            return by_name[name]

        def barrier():
            for q in (pe, dve, act, pool, sp):
                q(None, [(s.sem, s.count) for s in by_name.values() if s.count])

        gen_state = {"n": 0, "read": [None, None]}

        def take_bank():
            i = gen_state["n"] % 2
            gen_state["n"] += 1
            return i, general[i], gen_state["read"][i]

        def bank_read(i, event):
            gen_state["read"][i] = event

        ev_const = sp(lambda e: e.dma_start(consts[:, :], consts_in[:, 0:C_STAY]), signal=S("consts_loaded"), by=16)
        recast = att[:, 0:5, :].rearrange("p a c -> p (a c)")
        ev_recast = sp(lambda e: e.dma_start(recast[:, 0:C_END - C_STAY], consts_in[:, C_STAY:]),
                       signal=S("recast_loaded"), by=16)
        ev_vec = sp(lambda e: e.dma_start(vec[:, :], vec_in), signal=S("vec_loaded"), by=16)
        dve(lambda e: e.tensor_copy(mask_bf[:, :], recast[:, 0:C_SPREAD - C_MASK]), [ev_recast])
        dve(lambda e: e.tensor_copy(spread_sel[:, :], recast[:, C_SPREAD - C_MASK:C_END - C_STAY]))
        ev_bf = dve(lambda e: e.tensor_copy(ident_bf[:, :], ident), [ev_const], signal=S("bf16_consts"))
        ev_ones = pool(lambda e: e.memset(k_inv[:, 0:WIN], 1.0), signal=S("ones_set"))
        ev_zero = pool(lambda e: e.memset(xs[:, :, :], 0.0), signal=S("shift_zeroed"))

        staging = qk_ring[0]
        x_tiles = x_in.rearrange("b (h p) d -> p (b h) d", p=P)
        stage_v = staging[:, 0:4, :].rearrange("p r (h d) -> p (r h) d", d=P)
        ev_in = sp(lambda e: e.dma_start(stage_v, x_tiles), signal=S("x_loaded"), by=16)
        ev = None
        x_ready = [None] * CHUNKS
        for c in range(CHUNKS):
            i, g, free = take_bank()
            for j in range(4):
                ev = pe(lambda e, c=c, j=j, g=g: e.transpose(g[:, j * P:(j + 1) * P],
                        stage_v[:, 4 * c + j, :], ident), [free, ev_in, ev_const],
                        signal=S("x_turned") if j == 3 else None)
            x_ready[c] = dve(lambda e, c=c, g=g: e.tensor_copy(x[:, c * COLS:(c + 1) * COLS], g[:, :]),
                             [ev], signal=S("x_kept"))
            bank_read(i, x_ready[c])

        last = {"centered_read": None, "rstd_read": None, "var_t_read": None}

        def norm_center(src, ready):
            i, g, free = take_bank()
            ev = pe(lambda e: e.matmul(g[:, :], center, src, start=True, stop=True),
                    [free, ready], signal=S("ln_centered"))
            ev = dve(lambda e: e.tensor_copy(centered[:, :], g[:, :]),
                     [ev, last["centered_read"]], signal=S("ln_center_kept"))
            bank_read(i, ev)
            return pool(lambda e: e.tensor_tensor(rstd[:, :], centered[:, :], centered[:, :], ALU.mult),
                        [ev, last["rstd_read"]], signal=S("ln_squared"))

        def norm_var(squared):
            i, g, free = take_bank()
            ev = pe(lambda e: e.matmul(g[:, :], mean, rstd[:, :], start=True, stop=True),
                    [free, squared], signal=S("ln_var"))
            ev = dve(lambda e: e.tensor_scalar(rstd[:, :], g[:, :], EPS, None, ALU.add),
                     [ev], signal=S("ln_var_kept"))
            bank_read(i, ev)
            ev = dve(lambda e: e.transpose(var_t.rearrange("p w k -> p (w k)"), rstd[:, :]),
                     [ev, last["var_t_read"]], signal=S("ln_var_turned"))
            return dve(lambda e: e.reciprocal(var_t[:, :, 0:1], var_t[:, :, 0:1]), [ev], signal=S("ln_inv"))

        def norm_root(inv):
            ev = act(lambda e: e.activation(var_t[:, :, 0:1], var_t[:, :, 0:1], ACT.Sqrt), [inv],
                     signal=S("ln_rstd"))
            ev = dve(lambda e: e.transpose(rstd[:, :], var_t[:, :, 0:1].broadcast_to([P, ITEM_WINS, WIN])),
                     [ev], signal=S("ln_rstd_turned"))
            last["var_t_read"] = ev
            return ev

        def norm_apply(ev, dst, gain=None, bias=None, dst_free=()):
            to = dst if gain is None else centered[:, :]
            ev = pool(lambda e: e.tensor_tensor(to, centered[:, :], rstd[:, :], ALU.mult),
                      [ev, *dst_free], signal=S("ln_scaled"))
            last["rstd_read"] = last["centered_read"] = ev
            if gain is not None:
                ev = pool(lambda e: e.tensor_scalar(dst, centered[:, :], gain, bias, ALU.mult, ALU.add),
                          [ev], signal=S("ln_affine"))
                last["centered_read"] = ev
            return ev

        xs_read = [None] * CHUNKS

        def shift_tokens(c, ready, x_wait=None):
            src = x[:, c * COLS:(c + 1) * COLS].rearrange("p (s t) -> p s t", s=CHUNK_SEQS)
            dst = xs[:, c * CHUNK_SEQS:(c + 1) * CHUNK_SEQS, :]
            act(lambda e: e.activation(dst[0:64, :, :], src[0:64, :, :], ACT.Copy),
                [ready, xs_read[c], ev_zero])
            return act(lambda e: e.activation(dst[64:P, :, 1:SEQ], src[64:P, :, 0:SEQ - 1], ACT.Copy),
                       signal=S("shifted_tokens"))

        items = [(layer, c) for layer in range(DEPTH) for c in range(CHUNKS)]
        slot_free = {"wqk": [None] * PAIRS, "raw": [None, None], "wv": [None, None], "sin": [None, None],
                     "wo": None, "w1": None, "w2": None}
        w_ready = {}
        ring_read = [[None] * RING, [None] * RING]
        v_read = [None, None]
        att_read = [ev_bf] * PAIRS
        misc = {"squares": [None] * 4, "partner": [None, None], "proj": [None, None], "xs_parts": [None, None],
                "scores": None, "attp": [None, None], "sums_read": None, "inv_parts_read": None,
                "inv_read": None, "norm_t_read": None,
                "q_scale_read": [None, None], "k_inv_read": None, "probs_read": [None, None], "probs_t_read": [None, None],
                "hidden_read": None}
        vround = {"n": 0}

        def stack(xs_ready):
            state = {}
            x_state = list(xs_ready)

            def load_pair(layer, p):
                r = p % 2
                src = wqkv_in[layer].rearrange("d (k c) -> d k c", k=3)[:, 0:2, p * P:(p + 1) * P]
                raw = wqk_raw[:, r, :]
                ev = sp(lambda e: e.dma_start(raw.rearrange("d (k c) -> d k c", k=2), src),
                        [slot_free["raw"][r]], signal=S(f"wqk_raw{r}_loaded"), by=16)
                ev_hi = act(lambda e: e.activation(wqk_hi[:, p, :], raw, ACT.Copy), [ev, slot_free["wqk"][p]],
                            signal=S("wqk_hi_made"))
                ev_lo = dve(lambda e: e.tensor_tensor(wqk_lo[:, p, :], raw, wqk_hi[:, p, :].bitcast(F32),
                                                      ALU.subtract), [ev_hi], signal=S("wqk_lo_made"))
                slot_free["raw"][r] = ev_lo
                w_ready["wqk", layer, p] = ev_lo

            def load_tables(layer):
                for which in range(2):
                    w_ready["sin", layer, which] = pool(
                        lambda e, which=which: e.tensor_scalar(sin_scaled[:, which, :], tables[:, 2 * which + 1, :],
                        vcol(layer, V_QSR + 2 * which), None, ALU.mult),
                        [slot_free["sin"][which], ev_vec, ev_const], signal=S("sin_scaled"))

            def load_v(layer):
                i = vround["n"] % 2
                vround["n"] += 1
                w_ready["wv", layer] = (i, sp(lambda e: e.dma_start(wv[:, i, :], wqkv_in[layer][:, 2 * INNER:]),
                                              [slot_free["wv"][i]], signal=S(f"wv{i}_loaded"), by=16))

            def load_wo(layer):
                src = wo_in[layer].rearrange("(p d) n -> d p n", d=P)
                w_ready["wo", layer] = sp(lambda e: e.dma_start(wo[:, :, :], src), [slot_free["wo"]],
                                          signal=S("wo_loaded"), by=16)

            def load_w1(layer):
                w_ready["w1", layer] = sp(lambda e: e.dma_start(w1[:, :], w1_in[layer]), [slot_free["w1"]],
                                          signal=S("w1_loaded"), by=16)

            def load_w2(layer):
                full = len(HIDDEN_CUTS) - 1
                src = w2_in[layer][0:full * P, :].rearrange("(j d) n -> d j n", d=P)
                sp(lambda e: e.dma_start(w2[:, 0:full, :], src), [slot_free["w2"]],
                   signal=S("w2_loaded"), by=16)
                a, n = HIDDEN_CUTS[-1]
                w_ready["w2", layer] = sp(lambda e: e.dma_start(w2[0:n, full, :], w2_in[layer][a:a + n, :]),
                                          signal=S("w2_loaded"), by=16)

            def vcol(layer, i):
                return vec[:, layer * V_END + i:layer * V_END + i + 1]

            def split_tokens(n):
                c, r = items[n][1], n % 2
                src = xs[:, c * CHUNK_SEQS:(c + 1) * CHUNK_SEQS, :].rearrange("p s t -> p (s t)")
                ev = act(lambda e: e.activation(xs_hi[:, r, :], src, ACT.Copy), [x_state[c], misc["xs_parts"][r]],
                         signal=S("xs_hi_made"))
                state[n]["xs"] = dve(lambda e: e.tensor_tensor(xs_lo[:, r, :], src, xs_hi[:, r, :].bitcast(F32),
                                     ALU.subtract), [ev], signal=S("xs_lo_made"))

            def project(n, p, which):
                layer, r, g = items[n][0], n % 2, proj[which]
                cut = slice(which * P, (which + 1) * P)
                parts = [(wqk_lo, xs_hi), (wqk_hi, xs_lo), (wqk_hi, xs_hi)]
                for j, (w, y) in enumerate(parts):
                    pp = pe(lambda e, j=j, w=w, y=y: e.matmul(g[:, :], w[:, p, cut], y[:, r, :], start=(j == 0),
                            stop=(j == 2)), [state[n]["xs"], w_ready["wqk", layer, p], misc["proj"][which]],
                            signal=S("proj_done") if j == 2 else None)
                slot_free["wqk"][p] = misc["xs_parts"][r] = pp
                sq = (2 * p + which) % 4
                sq_ev = act(lambda e: e.activation(squares[:, sq, :], g[:, :], ACT.Square),
                            [pp, misc["squares"][sq]], signal=S("squared"))
                slot = (n * PAIRS + p) % RING
                y, other = qk_ring[which][:, slot, :], partner[:, which, :]

                def by_seq(a):
                    return a.rearrange("p (s t) -> p s t", s=CHUNK_SEQS)

                def both(a):
                    return a.unsqueeze(1).broadcast_to([P, CHUNK_SEQS, SEQ])

                ra = dve(lambda e: e.stream_shuffle(other, g[:, :], PARTNER), [sq_ev, misc["partner"][which]],
                         signal=S("partnered"))
                rb = dve(lambda e: e.scalar_tensor_tensor(out=by_seq(y), in0=by_seq(g[:, :]),
                         scalar=vcol(layer, V_QS + 2 * which), in1=both(tables[:, 2 * which, :]),
                         op0=ALU.mult, op1=ALU.mult), [ring_read[which][slot], ev_vec, ev_const],
                         signal=S("cos_done"))
                misc["proj"][which] = rb
                rc = pool(lambda e: e.tensor_tensor(by_seq(other), by_seq(other), both(sin_scaled[:, which, :]),
                                                    ALU.mult), [ra, w_ready["sin", layer, which]],
                          signal=S("sin_done"))
                slot_free["sin"][which] = rc
                done = pool(lambda e: e.tensor_tensor(y, y, other, ALU.add), [rb, rc], signal=S("rotated"))
                misc["partner"][which] = done
                state[n]["sq", p, which] = sq_ev
                state[n]["rot", p, which] = done

            def sum_squares(n, couple):
                for j in range(4):
                    p, which = 2 * couple + j // 2, j % 2
                    sel = consts[:, C_SUMSEL + 30 - 2 * couple:C_SUMSEL + 62 - 2 * couple]
                    wait = [state[n]["sq", p, which]]
                    if couple == 0:
                        wait += [misc["sums_read"], ev_const]
                    ev = pe(lambda e, j=j, sel=sel: e.matmul(sums[32 * j:32 * j + 32, :], sel,
                            squares[:, j, :], start=(couple == 0), stop=(couple == PAIRS // 2 - 1)),
                            wait, signal=S("squares_summed") if j == 3 else None)
                misc["squares"] = [ev] * 4
                state[n]["sums"] = ev

            def invert_norms(n):
                ev = dve(lambda e: e.tensor_scalar(inv_norm[:, :], sums[:, :], 1e-24, None, ALU.max),
                         [state[n]["sums"], misc["inv_read"]], signal=S("sums_kept"))
                misc["sums_read"] = ev
                ev = dve(lambda e: e.transpose(norm_t.rearrange("p w h -> p (w h)"), inv_norm[:, :]),
                         [ev, misc["norm_t_read"]], signal=S("sums_turned"))
                used = norm_t[:, :, 0:NORM_ROWS]
                ev = dve(lambda e: e.reciprocal(used, used), [ev], signal=S("sums_inverted"))
                state[n]["inverted"] = ev

            def root_norms(n):
                ev = state[n]["inverted"]
                used = norm_t[:, :, 0:NORM_ROWS]
                for g in range(4):
                    h, r0 = g % 2, 2 * WIN * (g // 2)
                    src = norm_t[r0:r0 + WIN, :, h:NORM_ROWS:2].rearrange("p w g -> p g w")
                    q_ev = act(lambda e, g=g, src=src: e.activation(q_scale8[WIN * g:WIN * g + WIN, n % 2, :, :],
                               src, ACT.Sqrt, scale=QK_SCALE * QK_SCALE), [ev, misc["q_scale_read"][n % 2]],
                               signal=S("q_scaled"))
                state[n]["q_scale"] = q_ev
                state[n]["k_root"] = act(lambda e: e.activation(used, used, ACT.Sqrt), [q_ev],
                                         signal=S("k_norms_inverted"))

            def turn_k_norms(n):
                ev = dve(lambda e: e.transpose(inv_norm[:, :], norm_t.rearrange("p w h -> p (w h)")),
                         [state[n]["k_root"]], signal=S("k_norms_turned"))
                misc["norm_t_read"] = state[n]["k_turned"] = ev

            def split_k_norms(n):
                ev = state[n]["k_turned"]
                ev = act(lambda e: e.activation(inv_hi[:, :], inv_norm[:, :], ACT.Copy),
                                         [ev, misc["inv_parts_read"]], signal=S("inv_hi_made"))
                state[n]["inv"] = misc["inv_read"] = dve(
                    lambda e: e.tensor_tensor(inv_lo[:, :], inv_norm[:, :], inv_hi[:, :].bitcast(F32), ALU.subtract),
                    [ev], signal=S("inv_lo_made"))

            def project_v(n, p):
                layer, c = items[n]
                i, g, free = take_bank()
                wi, wv_ready = w_ready["wv", layer]
                for w in range(2):
                    win = 2 * p + w
                    lhs = xs[:, c * CHUNK_SEQS + win // NWIN, (win % NWIN) * WIN:(win % NWIN + 1) * WIN]
                    for q in range(4):
                        rhs = wv[:, wi, :].rearrange("d (r g c) -> d g r c", g=4, c=DH)[:, q, :, :]
                        o = g[32 * q:32 * q + 32, w * 256:(w + 1) * 256]
                        ev = pe(lambda e, o=o, lhs=lhs, rhs=rhs: e.matmul(o, lhs, rhs, start=True, stop=True),
                                [free, wv_ready, x_state[c]],
                                signal=S("v_projected") if w == 1 and q == 3 else None)
                slot_free["wv"][wi] = ev
                xs_read[c] = ev
                to = v_buf[:, n % 2, 2 * p:2 * p + 2, :]
                ev = act(lambda e: e.activation(to, g[:, :].rearrange("p (w c) -> p w c", w=2), ACT.Copy),
                         [ev, v_read[n % 2]], signal=S("v_kept"))
                bank_read(i, ev)
                state[n]["v", p] = ev

            def spread_k_norms(n, group):
                i, g, free = take_bank()
                sel = spread_sel[:, group * P:(group + 1) * P]
                pe(lambda e: e.matmul(g[:, :], sel, inv_lo[:, :], start=True, stop=False),
                   [free, state[n]["inv"]])
                ev = pe(lambda e: e.matmul(g[:, :], sel, inv_hi[:, :], start=False, stop=True),
                        signal=S("norm_spread"))
                misc["inv_parts_read"] = ev
                ev = dve(lambda e: e.tensor_copy(k_inv[:, WIN:], g[:, :]), [ev, misc["k_inv_read"]],
                         signal=S("k_inv_kept"))
                bank_read(i, ev)
                state[n]["k_inv"] = ev

            def attend_scores(n, s):
                group, seq = s // CHUNK_SEQS, s % CHUNK_SEQS
                pe(lambda e: e.matmul(scores[:, :], ident_bf[:, :], mask_bf[:, :], start=True, stop=False,
                                      skip_group_check=True),
                   [misc["scores"], ev_bf] + [state[n]["rot", 2 * group + j, k] for j in range(2) for k in range(2)])
                for w in range(NWIN):
                    for h in range(4):
                        slot = (n * PAIRS + 2 * group + h // 2) % RING
                        r0 = DH * (h % 2)
                        t0 = seq * SEQ + w * WIN
                        back = WIN if w else 0
                        qw = qk_ring[0][r0:r0 + DH, slot, t0:t0 + WIN]
                        kw = qk_ring[1][r0:r0 + DH, slot, t0 - back:t0 + WIN]
                        o = scores[32 * h:32 * h + 32, w * 2 * WIN + WIN - back:(w + 1) * 2 * WIN]
                        end = w == NWIN - 1 and h == 3
                        ev = pe(lambda e, o=o, qw=qw, kw=kw: e.matmul(o, qw, kw, start=False, stop=True,
                                skip_group_check=True), signal=S("scored") if end else None)
                for j in range(2):
                    slot = (n * PAIRS + 2 * group + j) % RING
                    ring_read[0][slot] = ring_read[1][slot] = ev
                state[n]["scored", s] = ev

            def spread_keys(y):
                return y.unsqueeze(2).broadcast_to([P, NWIN, 2 * WIN])

            def attend_scale(n, s):
                group, seq = s // CHUNK_SEQS, s % CHUNK_SEQS
                b = s % 2
                s3 = scores[:, :].rearrange("p (w k) -> p w k", w=NWIN)

                y3 = probs[:, b, :].rearrange("p (w k) -> p w k", w=NWIN)
                start = k_inv[:, seq * SEQ:seq * SEQ + 1]
                keys = bass.AP(start.tensor, start.offset, [list(start.ap[0]), [WIN, NWIN], [1, 2 * WIN]])
                ev = dve(lambda e: e.tensor_tensor(y3, s3, keys, ALU.mult),
                         [state[n]["scored", s], misc["probs_read"][b], state[n]["k_inv"], ev_ones], signal=S("k_norms_off"))
                misc["scores"] = misc["k_inv_read"] = state[n]["k_scaled", s] = ev

            def attend_max(n, s):
                group, seq = s // CHUNK_SEQS, s % CHUNK_SEQS
                b = s % 2
                y3 = probs[:, b, :].rearrange("p (w k) -> p w k", w=NWIN)
                ev = state[n]["k_scaled", s]
                ev = dve(lambda e: e.tensor_reduce(row_max[:, b, :], y3, AX.X, ALU.max),
                         [ev], signal=S("row_max"))
                ev = dve(lambda e: e.tensor_tensor(y3, y3, spread_keys(row_max[:, b, :]), ALU.subtract),
                         [ev], signal=S("max_off"))
                wins = slice(seq * NWIN, (seq + 1) * NWIN)
                scale = q_scale8[:, n % 2, group, wins]
                state[n]["scaled", s] = misc["q_scale_read"][n % 2] = pool(
                    lambda e: e.tensor_tensor(y3, y3, spread_keys(scale), ALU.mult),
                    [ev, state[n]["q_scale"]], signal=S("q_norms_off"))

            def attend_exp(n, s):
                y = probs[:, s % 2, :]
                state[n]["exp", s] = act(lambda e: e.activation(y, y, ACT.Exp), [state[n]["scaled", s]],
                                         signal=S("exponent"))

            def attend_probs(n, s):
                b = s % 2

                def cube(y):
                    return y.rearrange("p (w k) -> p w k", w=NWIN)

                ev = dve(lambda e: e.tensor_reduce(row_sum[:, b, :], cube(probs[:, b, :]), AX.X, ALU.add),
                         [state[n]["exp", s]], signal=S("row_sum"))
                ev = dve(lambda e: e.reciprocal(row_sum[:, b, :], row_sum[:, b, :]), [ev], signal=S("row_inv"))
                state[n]["p", s] = pool(lambda e: e.tensor_tensor(cube(probs[:, b, :]), cube(probs[:, b, :]),
                                        spread_keys(row_sum[:, b, :]), ALU.mult), [ev], signal=S("probs_done"))

            def attend_turn(n, s):
                b = s % 2
                ev = dve(lambda e: e.transpose(probs_t[:, b, :], probs[:, b, :]),
                         [state[n]["p", s], misc["probs_t_read"][b]], signal=S("probs_turned"))
                misc["probs_read"][b] = ev
                state[n]["pt", s] = ev

            def attend_values(n, s, blocks, done):
                group, seq = s // CHUNK_SEQS, s % CHUNK_SEQS
                b = s % 2
                for kb in blocks:
                    width = 2 * WIN if kb < NWIN - 1 else WIN
                    for h in range(4):
                        lhs = v_buf[32 * h:32 * h + 32, n % 2, seq * NWIN + kb, group * DH:(group + 1) * DH]
                        rhs = probs_t[32 * h:32 * h + 32, b, kb * 64 + WIN:kb * 64 + WIN + width]
                        o = attp[h // 2][DH * (h % 2):DH * (h % 2) + DH, kb * WIN:kb * WIN + width]
                        end = kb == NWIN - 1 and h == 3
                        ev = pe(lambda e, o=o, lhs=lhs, rhs=rhs, kb=kb: e.matmul(o, lhs, rhs, start=(kb == 0),
                                stop=True, skip_group_check=True),
                                [state[n]["pt", s], state[n]["v", (seq + 1) * NWIN // 2 - 1], *misc["attp"]],
                                signal=S("valued") if end else None)
                if not done:
                    return
                misc["probs_t_read"][b] = ev
                v_read[n % 2] = ev
                for j in range(2):
                    to = att[:, 2 * group + j, seq * SEQ:(seq + 1) * SEQ]
                    k = act(lambda e, j=j, to=to: e.activation(to, attp[j][:, 0:SEQ], ACT.Copy),
                            [ev, att_read[2 * group + j]], signal=S("att_kept"))
                    misc["attp"][j] = k
                state[n]["att"] = k

            def project_out(n, pairs):
                layer, c = items[n]
                i, g, free = take_bank()
                for p in pairs:
                    ev = pe(lambda e, p=p: e.matmul(g[:, :], wo[:, p, :], att[:, p, :], start=(p == pairs[0]),
                                                    stop=(p == pairs[-1])),
                            [free, w_ready["wo", layer], state[n]["att"]],
                            signal=S("out_projected") if p == pairs[-1] else None)
                for p in pairs:
                    att_read[p] = ev
                slot_free["wo"] = ev
                xc = x[:, c * COLS:(c + 1) * COLS]
                ev = dve(lambda e: e.tensor_tensor(xc, xc, g[:, :], ALU.add), [ev, x_state[c]],
                         signal=S("att_added"))
                bank_read(i, ev)
                if pairs[-1] < PAIRS - 1:
                    x_state[c] = ev
                    return
                x_state[c] = shift_tokens(c, ev)
                if c == CHUNKS - 1 and layer + 1 < DEPTH:
                    load_wo(layer + 1)

            def ffn_center(n):
                c = items[n][1]
                rhs = xs[:, c * CHUNK_SEQS:(c + 1) * CHUNK_SEQS, :]
                state[n]["lnsq"] = norm_center(rhs, x_state[c])
                xs_read[c] = (S("ln_centered").sem, S("ln_centered").count)

            def ffn_var(n):
                state[n]["lninv"] = norm_var(state[n]["lnsq"])

            def ffn_root(n):
                state[n]["lnroot"] = norm_root(state[n]["lninv"])

            def ffn_norm(n):
                layer = items[n][0]
                state[n]["xn"] = norm_apply(state[n]["lnroot"], centered[:, :], vcol(layer, V_G), vcol(layer, V_B))

            def ffn_gate(n, j):
                layer = items[n][0]
                a, m = HIDDEN_CUTS[j]
                i, g, free = take_bank()
                ev = pe(lambda e: e.matmul(g[0:m, :], w1[:, HIDDEN + a:HIDDEN + a + m], centered[:, :],
                        start=True, stop=True), [free, w_ready["w1", layer], state[n]["xn"]], signal=S("gate_done"))
                ev = act(lambda e: e.activation(hidden[0:m, j, :], g[0:m, :], ACT.Gelu,
                         bias=vcol(layer, V_BG + j)[0:m, :]), [ev, misc["hidden_read"]], signal=S("gelu_done"))
                bank_read(i, ev)
                state[n]["gate", j] = ev

            def ffn_value(n, j):
                layer = items[n][0]
                a, m = HIDDEN_CUTS[j]
                i, g, free = take_bank()
                ev = pe(lambda e: e.matmul(g[0:m, :], w1[:, a:a + m], centered[:, :], start=True, stop=True),
                        [free], signal=S("value_done"))
                last["centered_read"] = slot_free["w1"] = ev
                ev = dve(lambda e: e.scalar_tensor_tensor(out=hidden[0:m, j, :], in0=g[0:m, :],
                         scalar=vcol(layer, V_BA + j)[0:m, :], in1=hidden[0:m, j, :], op0=ALU.add, op1=ALU.mult),
                         [ev, state[n]["gate", j]], signal=S("hidden_done"))
                bank_read(i, ev)
                state[n]["hidden"] = ev
                if j == len(HIDDEN_CUTS) - 1 and items[n][1] == CHUNKS - 1 and layer + 1 < DEPTH:
                    load_w1(layer + 1)

            def ffn_out(n):
                layer, c = items[n]
                i, g, free = take_bank()
                for j, (a, m) in enumerate(HIDDEN_CUTS):
                    ev = pe(lambda e, j=j, m=m: e.matmul(g[:, :], w2[0:m, j, :], hidden[0:m, j, :],
                            start=(j == 0), stop=(j == len(HIDDEN_CUTS) - 1)),
                            [free, w_ready["w2", layer], state[n]["hidden"]],
                            signal=S("ffn_done") if j == len(HIDDEN_CUTS) - 1 else None)
                misc["hidden_read"] = slot_free["w2"] = ev
                xc = x[:, c * COLS:(c + 1) * COLS]
                ev = dve(lambda e: e.scalar_tensor_tensor(out=xc, in0=g[:, :], scalar=vcol(layer, V_B2), in1=xc,
                         op0=ALU.add, op1=ALU.add), [ev, x_state[c]], signal=S("ffn_added"))
                bank_read(i, ev)
                x_state[c] = shift_tokens(c, ev)
                if c == CHUNKS - 1 and layer + 1 < DEPTH:
                    load_w2(layer + 1)

            load_v(0)
            load_tables(0)
            for p in range(PAIRS):
                load_pair(0, p)
            load_wo(0)
            load_w1(0)
            load_w2(0)
            N = len(items)
            early = {4: [lambda n: project_out(n, (4, 5, 6, 7))], 5: [ffn_center], 7: [ffn_root, ffn_norm], 11: [ffn_out]}
            middle = {}
            for j in range(len(HIDDEN_CUTS)):
                middle[8 + j] = [lambda n, j=j: ffn_gate(n, j)]
            late = {8 + j: [lambda n, j=j: ffn_value(n, j)] for j in range(len(HIDDEN_CUTS))}
            after_k = {-3: [lambda n: project_out(n, (0, 1))], -1: [lambda n: project_out(n, (2, 3))]}
            end = {6: [ffn_var]}

            def stage_c(t, pieces):
                for k, stages in pieces.items():
                    n = (t - k) // SUBSTEPS - 2
                    if (t - k) % SUBSTEPS == 0 and 0 <= n < N:
                        for stage in stages:
                            stage(n)

            def at(t, lag):
                n, p = divmod(t - lag, SUBSTEPS)
                return (n, p) if 0 <= n < N else None

            for t in range(SUBSTEPS * (N + 3) + 6):
                n, p = divmod(t, SUBSTEPS)
                now = at(t, 0)
                if p == 0 and now and n and items[n][1] == 0:
                    load_tables(items[n][0])
                stage_c(t, early)
                norms_due = p == 1 and 0 <= n - 1 < N
                if norms_due:
                    invert_norms(n - 1)
                if scores_at := at(t, SCORES_LAG):
                    attend_scores(*scores_at)
                if p % 2 == 0:
                    m, couple = (n, p // 2 - 1) if p else (n - 1, PAIRS // 2 - 1)
                    if 0 <= m < N and couple >= 0:
                        sum_squares(m, couple)
                if now:
                    if t == 0:
                        state[0] = {}
                        split_tokens(0)
                    project(n, p, 0)
                if scores_at and p % 2 == 0:
                    spread_k_norms(scores_at[0], scores_at[1] // 2)
                if v_at := at(t, V_LAG):
                    project_v(*v_at)
                if norms_due:
                    root_norms(n - 1)
                if scores_at:
                    attend_scale(*scores_at)
                if probs_at := at(t, PROBS_LAG):
                    attend_probs(*probs_at)
                if scores_at:
                    attend_max(*scores_at)
                if norms_due:
                    turn_k_norms(n - 1)
                if values_at := at(t, VALUES_LAG):
                    attend_values(*values_at, range(0, NWIN // 2), False)
                stage_c(t, middle)
                stage_c(t, late)
                if values_at:
                    attend_values(*values_at, range(NWIN // 2, NWIN), True)
                if norms_due:
                    split_k_norms(n - 1)
                if now:
                    project(n, p, 1)
                stage_c(t, after_k)
                if probs_at:
                    attend_turn(*probs_at)
                if scores_at:
                    attend_exp(*scores_at)
                stage_c(t, end)
                if now:
                    layer, c = items[n]
                    if c == CHUNKS - 1 and layer + 1 < DEPTH:
                        load_pair(layer + 1, p)
                        if p == 0:
                            load_v(layer + 1)
                if now and n < N - 1 and p == SUBSTEPS - 2:
                    state[n + 1] = {}
                    split_tokens(n + 1)
            return x_state

        def layer_norm(c, ready, dst, gain=None, bias=None):
            sq = norm_center(x[:, c * COLS:(c + 1) * COLS], ready)
            return norm_apply(norm_root(norm_var(sq)), dst, gain, bias)

        def half_step(ready, load_first):
            stored = [sp(lambda e, c=c: e.dma_start(base_dram[:, c * COLS:(c + 1) * COLS],
                      x[:, c * COLS:(c + 1) * COLS]), [ready[c]], signal=S("base_stored"), by=16)
                      for c in range(CHUNKS)]
            xs_ready = []
            for c in range(CHUNKS):
                ev = layer_norm(c, ready[c], x[:, c * COLS:(c + 1) * COLS]) if False else None
                sq = norm_center(x[:, c * COLS:(c + 1) * COLS], ready[c])
                ev = norm_apply(norm_root(norm_var(sq)), x[:, c * COLS:(c + 1) * COLS], dst_free=[stored[-1]])
                xs_ready.append(shift_tokens(c, ev))
            ends = stack(xs_ready)
            done = []
            for c in range(CHUNKS):
                base = qk_ring[0][:, c, :]
                ev = sp(lambda e, c=c, base=base: e.dma_start(base, base_dram[:, c * COLS:(c + 1) * COLS]),
                        [stored[-1], *ring_read[0]], signal=S(f"base{c}_loaded"), by=16)
                xc = x[:, c * COLS:(c + 1) * COLS]
                done.append(dve(lambda e, xc=xc, base=base: e.scalar_tensor_tensor(out=xc, in0=xc, scalar=0.5,
                            in1=base, op0=ALU.mult, op1=ALU.add), [ev, ends[c]], signal=S("half_added")))
                for w in (0, 1):
                    ring_read[w] = [done[-1]] * RING
            return done

        def scan_block():
            barrier()
            pool_a = [qk_ring[0][:, i, :] for i in range(RING)]
            pool_b = [qk_ring[1][:, i, :] for i in range(RING)]
            xn, u, z, dt, dtu, acc, e1, ln1, gate, corr = pool_a[:10]
            decay = [pool_b[0], pool_b[1]]
            drive = [pool_b[2], pool_b[3]]
            hstate = [pool_b[4], pool_b[5]]
            hc = [pool_b[6], pool_b[7]]
            padded = v_buf[:, 0, 0:3, :].rearrange("p w c -> p (w c)")[:, 0:CHUNK_SEQS * (SEQ + 2)]\
                .rearrange("p (s t) -> p s t", s=CHUNK_SEQS)
            mw = v_buf[:, 1, 0:2, :].rearrange("p w c -> p (w c)")[:, 0:4 * P].rearrange("p (m n) -> p m n", m=4)
            wbc = v_buf[:, 1, 2, 0:2 * STATES]
            mvec = v_buf[:, 1, 3, 0:M_END]
            neg_a = v_buf[:, 1, 4, 0:STATES]

            def mcol(i):
                return mvec[:, i:i + 1]

            sp(lambda e: e.dma_start(mw, mw_in.rearrange("m d n -> d m n")), signal=S("m_loaded"), by=16)
            sp(lambda e: e.dma_start(wbc, wb_in), signal=S("m_loaded"), by=16)
            ev_m = sp(lambda e: e.dma_start(mvec, mvec_in), signal=S("m_loaded"), by=16)
            act(lambda e: e.activation(neg_a, mvec[:, M_ALOG:M_ALOG + STATES], ACT.Exp), [ev_m],
                signal=S("m_a"))
            ev_a = act(lambda e: e.mul(neg_a, neg_a, -1.0), [(S("m_a").sem, S("m_a").count)], signal=S("m_a"))
            ev_pad = pool(lambda e: e.memset(padded, 0.0), signal=S("m_pad"))
            acc_read = dtu_read = None
            rd = {"drive": [None, None], "hc": [None, None], "h": [None, None], "decay": [None, None]}
            done = []
            chain = S("m_dve")

            def D(make, after=()):
                return dve(make, [*after, (chain.sem, chain.count)] if chain.count else after, signal=chain)

            for c in range(CHUNKS):
                xc = x[:, c * COLS:(c + 1) * COLS]
                prev = done[-1] if done else None
                ev = layer_norm(c, prev, xn)
                sq = norm_center(xn, ev)
                ev = norm_apply(norm_root(norm_var(sq)), xn, mcol(M_G), mcol(M_B))

                def linear(m, rhs, ready):
                    i, g, free = take_bank()
                    return i, g, pe(lambda e: e.matmul(g[:, :], mw[:, m, :], rhs, start=True, stop=True),
                                    [free, ready, ev_m], signal=S("m_linear"))

                ev_xn = ev
                i, g, ev = linear(0, xn, ev_xn)
                g3 = g[:, :].rearrange("p (s t) -> p s t", s=CHUNK_SEQS)
                ev = D(lambda e, g3=g3: e.tensor_scalar(padded[:, :, 1:SEQ + 1], g3, mcol(M_W1B), None, ALU.add),
                       [ev, ev_pad])
                bank_read(i, ev)
                u3 = u.rearrange("p (s t) -> p s t", s=CHUNK_SEQS)
                D(lambda e: e.tensor_scalar(u3, padded[:, :, 0:SEQ], mcol(M_CONV), None, ALU.mult), [ev_m])
                D(lambda e: e.scalar_tensor_tensor(out=u3, in0=padded[:, :, 1:SEQ + 1], scalar=mcol(M_CONV + 1),
                  in1=u3, op0=ALU.mult, op1=ALU.add))
                ev = D(lambda e: e.scalar_tensor_tensor(out=u3, in0=padded[:, :, 2:SEQ + 2], scalar=mcol(M_CONV + 2),
                       in1=u3, op0=ALU.mult, op1=ALU.add))
                ev_u = act(lambda e: e.activation(u, u, ACT.Silu), [ev], signal=S("m_u"))
                i, g, ev = linear(1, xn, ev_xn)
                ev_gate = act(lambda e, g=g: e.activation(gate, g[:, :], ACT.Silu, bias=mcol(M_V1B)), [ev],
                              signal=S("m_gate"))
                bank_read(i, ev_gate)
                i, g, ev = linear(2, u, ev_u)
                ev = D(lambda e, g=g: e.tensor_scalar(z, g[:, :], mcol(M_BDT), None, ALU.add), [ev])
                bank_read(i, ev)
                ev = D(lambda e: e.scalar_tensor_tensor(out=e1, in0=z, scalar=-1.0, in1=z, op0=ALU.mult, op1=ALU.min))
                ev = act(lambda e: e.activation(e1, e1, ACT.Exp), [ev], signal=S("m_exp"))
                ev_w = D(lambda e: e.tensor_scalar(corr, e1, 1.0, None, ALU.add), [ev])
                ev_l = act(lambda e: e.activation(ln1, corr, ACT.Ln), [ev_w], signal=S("m_ln"))
                D(lambda e: e.scalar_tensor_tensor(out=corr, in0=corr, scalar=1.0, in1=e1, op0=ALU.subtract,
                  op1=ALU.subtract), [ev_l])
                D(lambda e: e.tensor_tensor(ln1, ln1, corr, ALU.subtract))
                ev_dt = D(lambda e: e.scalar_tensor_tensor(out=dt, in0=z, scalar=0.0, in1=ln1, op0=ALU.max,
                          op1=ALU.add))
                ev_dtu = D(lambda e: e.tensor_tensor(dtu, dt, u, ALU.mult), [ev_u])
                ev_acc = pool(lambda e: e.tensor_scalar(acc, u, mcol(M_D), None, ALU.mult), [ev_u, acc_read],
                              signal=S("m_acc"))
                for s in range(STATES):
                    b = s % 2
                    ev_dec = act(lambda e, s=s, b=b: e.activation(decay[b], dt, ACT.Exp, scale=neg_a[:, s:s + 1]),
                                 [ev_dt, ev_a, rd["decay"][b]], signal=S("m_decay"))
                    i, g, free = take_bank()
                    ev = pe(lambda e, s=s, g=g: e.matmul(g[:, :], wbc[:, s:s + 1].broadcast_to([P, P]), u,
                            start=True, stop=True), [free, ev_u, ev_m], signal=S("m_b"))
                    ev = dve(lambda e, b=b, g=g: e.tensor_tensor(drive[b], dtu, g[:, :], ALU.mult),
                             [ev, ev_dtu, rd["drive"][b]], signal=S("m_drive"))
                    bank_read(i, ev)
                    for q in range(CHUNK_SEQS):
                        cut = slice(q * SEQ, (q + 1) * SEQ)
                        ev_h = dve(lambda e, b=b, cut=cut: e.tensor_tensor_scan(hstate[b][:, cut], decay[b][:, cut],
                                   drive[b][:, cut], 0.0, ALU.mult, ALU.add), [ev, ev_dec, rd["h"][b]],
                                   signal=S("m_scan"))
                    rd["decay"][b] = rd["drive"][b] = ev_h
                    i, g, free = take_bank()
                    ev = pe(lambda e, s=s, g=g: e.matmul(g[:, :], wbc[:, STATES + s:STATES + s + 1].broadcast_to([P, P]),
                            u, start=True, stop=True), [free], signal=S("m_c"))
                    ev = dve(lambda e, b=b, g=g: e.tensor_tensor(hc[b], hstate[b], g[:, :], ALU.mult),
                             [ev, ev_h, rd["hc"][b]], signal=S("m_hc"))
                    rd["h"][b] = ev
                    bank_read(i, ev)
                    ev_acc = pool(lambda e, b=b: e.tensor_tensor(acc, acc, hc[b], ALU.add), [ev, ev_acc],
                                  signal=S("m_acc"))
                    rd["hc"][b] = ev_acc
                ev = D(lambda e: e.tensor_tensor(acc, acc, gate, ALU.mult), [ev_acc, ev_gate])
                i, g, ev = linear(3, acc, ev)
                acc_read = ev
                ev = D(lambda e, g=g, xc=xc: e.scalar_tensor_tensor(out=xc, in0=g[:, :], scalar=mcol(M_W2B), in1=xc,
                       op0=ALU.add, op1=ALU.add), [ev])
                bank_read(i, ev)
                done.append(ev)
            barrier()
            return done

        ready = half_step(x_ready, True)
        ready = scan_block()
        ready = half_step(ready, False)

        barrier()
        out_tiles = out.rearrange("b (h p) d -> p (b h) d", p=P)
        stage_out = qk_ring[1][:, 0:4, :].rearrange("p r (h d) -> p (r h) d", d=P)
        for c in range(CHUNKS):
            i, g, free = take_bank()
            for j in range(4):
                ev = pe(lambda e, c=c, j=j, g=g: e.transpose(g[:, j * P:(j + 1) * P],
                        x[:, (4 * c + j) * P:(4 * c + j + 1) * P], ident), [free, ready[c]],
                        signal=S("out_turned") if j == 3 else None)
            ev = dve(lambda e, c=c, g=g: e.tensor_copy(stage_out[:, 4 * c:4 * c + 4, :],
                     g[:, :].rearrange("p (h d) -> p h d", d=P)), [ev], signal=S("out_kept"))
            bank_read(i, ev)
            ev_out = sp(lambda e, c=c: e.dma_start(out_tiles[:, 4 * c:4 * c + 4, :], stage_out[:, 4 * c:4 * c + 4, :]),
                        [ev], signal=S("out_stored"), by=16)
        sp(None, [ev_out])

        block = ctx.enter_context(nc.Block())

        @block.sync
        def _(e):
            sp.run(e)

        @block.tensor
        def _(e):
            pe.run(e)

        @block.vector
        def _(e):
            dve.run(e)

        @block.scalar
        def _(e):
            act.run(e)

        @block.gpsimd
        def _(e):
            pool.run(e)


def constants():
    f = np.float32
    c = np.zeros((P, C_END), f)
    c[:, C_IDENT:C_IDENT + P] = np.eye(P, dtype=f)
    c[:, C_CENTER:C_CENTER + P] = np.eye(P, dtype=f) - f(1 / P)
    c[:, C_MEAN] = f(1 / P)
    c[np.arange(P), C_SUMSEL + 30 + np.arange(P) // DH] = 1
    half = np.arange(0, DH, 2, dtype=f)
    inv_freq = (f(1) / f(10000) ** (half / f(DH))).astype(f)
    t = np.arange(SEQ, dtype=f)
    freqs = t[:, None] * inv_freq[None, :]
    freqs = np.concatenate([freqs, freqs], -1)
    base = ((half + f(0.4 * DH)) / f(1.4 * DH)).astype(f)
    power = ((t - SEQ // 2) / f(WIN // 2)).astype(f)
    scale = base[None, :] ** power[:, None]
    scale = np.concatenate([scale, scale], -1).astype(f)
    inv = (f(1) / scale).astype(f)
    sign = np.where(np.arange(DH) < DH // 2, f(-1), f(1))
    tables = [np.cos(freqs) * scale, np.sin(freqs) * scale * sign, np.cos(freqs) * inv, np.sin(freqs) * inv * sign]
    for i, y in enumerate(tables):
        c[:, C_TABLES + i * SEQ:C_TABLES + (i + 1) * SEQ] = np.tile(y.T[HEAD_ORDER].astype(f), (2, 1))
    i = np.arange(P)[:, None, None] % WIN
    w = np.arange(NWIN)[None, :, None]
    j = np.arange(2 * WIN)[None, None, :]
    seen = np.where(j < WIN, (j >= i) & (w > 0), j - WIN <= i)
    c[:, C_MASK:C_SPREAD] = np.where(seen, f(0), f(-1e30)).reshape(P, -1)
    for head in range(HEADS):
        c[norm_row(head // 2, 1) + head % 2, C_SPREAD + head * WIN:C_SPREAD + (head + 1) * WIN] = 1
    return c


def kernel(**inputs):
    import concourse.bacc as bacc
    from concourse.bass_utils import run_bass_kernel_spmd

    a = {k: np.ascontiguousarray(v) for k, v in inputs.items()}
    vec = np.zeros((P, DEPTH, V_END), np.float32)
    for at, name in ((V_QS, "q_scale"), (V_KS, "k_scale")):
        s = a["L0_ffn_" + name]
        swapped = np.concatenate([s[:, DH // 2:], s[:, :DH // 2]], 1)
        vec[:, :, at] = np.concatenate([s[:, HEAD_ORDER]] * 2, 1).T
        vec[:, :, at + 1] = np.concatenate([swapped[:, HEAD_ORDER]] * 2, 1).T
    vec[:, :, V_G], vec[:, :, V_B], vec[:, :, V_B2] = a["L0_ffn_ln_g"].T, a["L0_ffn_ln_b"].T, a["L0_ffn_b2"].T
    for j, (s, n) in enumerate(HIDDEN_CUTS):
        vec[:n, :, V_BA + j] = a["L0_ffn_b1"][:, s:s + n].T
        vec[:n, :, V_BG + j] = a["L0_ffn_b1"][:, HIDDEN + s:HIDDEN + s + n].T
    m = "L0_attn_"
    mvec = np.concatenate([np.stack([a[m + k] for k in ("ln_g", "ln_b", "w1_b", "v1_b", "w2_b", "D_skip", "b_dt")], 1),
                           a[m + "conv_w"][:, 0, :], a[m + "A_log"]], 1)
    wqkv = a["L0_ffn_Wqkv"].reshape(DEPTH, P, 3, HEADS, DH)
    wqkv = np.concatenate([wqkv[:, :, 0:2][..., HEAD_ORDER], wqkv[:, :, 2:3]], 2).reshape(DEPTH, P, 3 * INNER)
    arrays = {
        "x": a[m + "x"], "consts": constants(), "vec": vec.reshape(P, -1), "mvec": np.ascontiguousarray(mvec),
        "wqkv": wqkv, "wo": a["L0_ffn_Wo"], "w1": a["L0_ffn_W1"], "w2": a["L0_ffn_W2"],
        "mw": np.stack([a[m + k] for k in ("w1_w", "v1_w", "W_dt", "w2_w")]),
        "wb": np.ascontiguousarray(np.concatenate([a[m + "W_B"], a[m + "W_C"]], 1)),
    }
    nc = bacc.Bacc("TRN2", target_bir_lowering=False, num_devices=1)
    args = [nc.dram_tensor(f"in_{k}", v.shape, mybir.dt.from_np(v.dtype), kind="ExternalInput").ap() for k, v in arrays.items()]
    out = nc.dram_tensor("out", a[m + "x"].shape, F32, kind="ExternalOutput").ap()
    macaron_kernel(nc, *args, out)
    r = run_bass_kernel_spmd(nc, [{f"in_{k}": v for k, v in arrays.items()}], core_ids=[0])
    return r.results[0]["out"]
```

```python
from contextlib import ExitStack

import numpy as np

import concourse.bass as bass
from concourse import mybir

F32 = mybir.dt.float32
BF16 = mybir.dt.bfloat16
F32R = mybir.dt.float32r
ALU = mybir.AluOpType
ACT = mybir.ActivationFunctionType
AX = mybir.AxisListType

P = 128
BATCH, SEQ = 8, 256
HEADS, DH = 16, 64
PAIRS = HEADS // 2
WIN = 32
NWIN = SEQ // WIN
CHUNK_SEQS = 2
COLS = CHUNK_SEQS * SEQ
CHUNKS = BATCH // CHUNK_SEQS
TOKENS = BATCH * SEQ
DEPTH = 6
INNER = HEADS * DH
HIDDEN = int(P * 4 * 2 / 3)
HIDDEN_CUTS = [(a, min(P, HIDDEN - a)) for a in range(0, HIDDEN, P)]
STATES = 16
QK_SCALE = 8.0
EPS = 1e-5
SUBSTEPS = PAIRS
RING = 12
SCORES_LAG = SUBSTEPS + 2
PROBS_LAG = SCORES_LAG + 1
VALUES_LAG = SCORES_LAG + 2
V_LAG = 5
GROUPS = HEADS // 4
ITEM_WINS = CHUNK_SEQS * NWIN
NORM_ROWS = 2 * GROUPS

C_IDENT, C_CENTER, C_MEAN, C_SUMSEL = 0, P, 2 * P, 2 * P + 1
C_TABLES = C_SUMSEL + 64
C_STAY = C_TABLES + 4 * SEQ
C_MASK = C_STAY
C_SPREAD = C_MASK + NWIN * 2 * WIN
C_END = C_SPREAD + GROUPS * P
HEAD_ORDER = [32 * f + 16 * q + r for q in range(2) for f in range(2) for r in range(16)]
PARTNER = [(i + 16) % 32 for i in range(32)]
V_QS, V_QSR, V_KS, V_KSR, V_G, V_B, V_B2, V_BA, V_BG, V_END = 0, 1, 2, 3, 4, 5, 6, 7, 10, 13
M_G, M_B, M_W1B, M_V1B, M_W2B, M_D, M_BDT, M_CONV, M_ALOG, M_END = 0, 1, 2, 3, 4, 5, 6, 7, 10, 26


def norm_row(p, which):
    return 32 * (2 * (p % 2) + which) + 2 * (p // 2)


class Signal:

    def __init__(self, sem):
        self.sem, self.count = sem, 0

    def next(self, by=1):
        self.count += by
        return (self.sem, self.count)


class Queue:

    def __init__(self):
        self.ops, self.seen = [], {}

    def __call__(self, make, after=(), signal=None, by=1):
        for event in after:
            if event is None:
                continue
            sem, value = event
            if self.seen.get(sem, 0) < value:
                self.seen[sem] = value
                self.ops.append(lambda e, s=sem, v=value: e.wait_ge(s, v))
        if make is None:
            return None
        if signal is None:
            self.ops.append(make)
            return None
        event = signal.next(by)
        self.ops.append(lambda e: make(e).then_inc(signal.sem, by))
        return event

    def run(self, e):
        for op in self.ops:
            op(e)


def macaron_kernel(nc, x_in, consts_in, vec_in, mvec_in, wqkv_in, wo_in, w1_in, w2_in,
                   mw_in, wb_in, out):
    ctx = ExitStack()
    with ctx:
        def sb(name, shape, dt=F32):
            return ctx.enter_context(nc.sbuf_tensor(name, shape, dt))

        def bank(name):
            return ctx.enter_context(nc.psum_tensor(name, [P, COLS], F32))

        def sig(name):
            return Signal(ctx.enter_context(nc.semaphore(name)))

        consts = sb("consts", [P, C_STAY])
        ident = consts[:, C_IDENT:C_IDENT + P]
        center = consts[:, C_CENTER:C_CENTER + P]
        mean = consts[:, C_MEAN:C_MEAN + 1].broadcast_to([P, P])
        tables = consts[:, C_TABLES:C_TABLES + 4 * SEQ].rearrange("p (i t) -> p i t", i=4)
        sin_scaled = sb("sin_scaled", [P, 2, SEQ])
        mask_bf = sb("mask_bf", [P, NWIN * 2 * WIN], BF16)
        ident_bf = sb("ident_bf", [P, P], BF16)
        vec = sb("vec", [P, DEPTH * V_END])
        x = sb("x", [P, TOKENS])
        xs = sb("xs", [P, BATCH, SEQ])
        wqk_raw = sb("wqk_raw", [P, 2, 2 * P])
        wqk_hi = sb("wqk_hi", [P, PAIRS, 2 * P], F32R)
        wqk_lo = sb("wqk_lo", [P, PAIRS, 2 * P], F32R)
        xs_hi = sb("xs_hi", [P, 2, COLS], F32R)
        xs_lo = sb("xs_lo", [P, 2, COLS], F32R)
        spread_sel = sb("spread_sel", [P, GROUPS * P], F32R)
        wv = sb("wv", [P, 2, INNER])
        wo = sb("wo", [P, PAIRS, P])
        w1 = sb("w1", [P, 2 * HIDDEN])
        w2 = sb("w2", [P, len(HIDDEN_CUTS), P])
        qk_ring = [sb("q_ring", [P, RING, COLS]), sb("k_ring", [P, RING, COLS])]
        v_buf = sb("v_buf", [P, 2, 2 * NWIN, 4 * DH])
        squares = sb("squares", [P, 4, COLS])
        partner = sb("partner", [P, 2, COLS])
        inv_norm = sb("inv_norm", [P, COLS])
        norm_t = sb("norm_t", [P, ITEM_WINS, WIN])
        q_scale8 = sb("q_scale8", [P, 2, GROUPS, ITEM_WINS])
        k_inv = sb("k_inv", [P, WIN + COLS])
        inv_hi, inv_lo = sb("inv_hi", [P, COLS], F32R), sb("inv_lo", [P, COLS], F32R)
        att = sb("att", [P, PAIRS, COLS])
        row_max = sb("row_max", [P, 2, NWIN])
        row_sum = sb("row_sum", [P, 2, NWIN])
        probs = sb("probs", [P, 2, COLS])
        probs_t = sb("probs_t", [P, 2, COLS])
        centered = sb("centered", [P, COLS])
        rstd = sb("rstd", [P, COLS])
        var_t = sb("var_t", [P, ITEM_WINS, WIN])
        hidden = sb("hidden", [P, len(HIDDEN_CUTS), COLS])
        base_dram = nc.dram_tensor("base_dram", [P, TOKENS], F32).ap()

        proj = [bank("proj_q"), bank("proj_k")]
        scores = bank("scores")
        attp = [bank("attp0"), bank("attp1")]
        sums = bank("sums")
        general = [bank("general0"), bank("general1")]

        pe, dve, act, pool, sp = Queue(), Queue(), Queue(), Queue(), Queue()
        by_name = {}

        def S(name):
            if name not in by_name:
                by_name[name] = sig(name)
            return by_name[name]

        def barrier():
            for q in (pe, dve, act, pool, sp):
                q(None, [(s.sem, s.count) for s in by_name.values() if s.count])

        gen_state = {"n": 0, "read": [None, None]}

        def take_bank():
            i = gen_state["n"] % 2
            gen_state["n"] += 1
            return i, general[i], gen_state["read"][i]

        def bank_read(i, event):
            gen_state["read"][i] = event

        ev_const = sp(lambda e: e.dma_start(consts[:, :], consts_in[:, 0:C_STAY]), signal=S("consts_loaded"), by=16)
        recast = att[:, 0:5, :].rearrange("p a c -> p (a c)")
        ev_recast = sp(lambda e: e.dma_start(recast[:, 0:C_END - C_STAY], consts_in[:, C_STAY:]),
                       signal=S("recast_loaded"), by=16)
        ev_vec = sp(lambda e: e.dma_start(vec[:, :], vec_in), signal=S("vec_loaded"), by=16)
        dve(lambda e: e.tensor_copy(mask_bf[:, :], recast[:, 0:C_SPREAD - C_MASK]), [ev_recast])
        dve(lambda e: e.tensor_copy(spread_sel[:, :], recast[:, C_SPREAD - C_MASK:C_END - C_STAY]))
        ev_bf = dve(lambda e: e.tensor_copy(ident_bf[:, :], ident), [ev_const], signal=S("bf16_consts"))
        ev_ones = pool(lambda e: e.memset(k_inv[:, 0:WIN], 1.0), signal=S("ones_set"))
        ev_zero = pool(lambda e: e.memset(xs[:, :, :], 0.0), signal=S("shift_zeroed"))

        staging = qk_ring[0]
        x_tiles = x_in.rearrange("b (h p) d -> p (b h) d", p=P)
        stage_v = staging[:, 0:4, :].rearrange("p r (h d) -> p (r h) d", d=P)
        ev_in = sp(lambda e: e.dma_start(stage_v, x_tiles), signal=S("x_loaded"), by=16)
        ev = None
        x_ready = [None] * CHUNKS
        for c in range(CHUNKS):
            i, g, free = take_bank()
            for j in range(4):
                ev = pe(lambda e, c=c, j=j, g=g: e.transpose(g[:, j * P:(j + 1) * P],
                        stage_v[:, 4 * c + j, :], ident), [free, ev_in, ev_const],
                        signal=S("x_turned") if j == 3 else None)
            x_ready[c] = dve(lambda e, c=c, g=g: e.tensor_copy(x[:, c * COLS:(c + 1) * COLS], g[:, :]),
                             [ev], signal=S("x_kept"))
            bank_read(i, x_ready[c])

        last = {"centered_read": None, "rstd_read": None, "var_t_read": None}

        def norm_center(src, ready):
            i, g, free = take_bank()
            ev = pe(lambda e: e.matmul(g[:, :], center, src, start=True, stop=True),
                    [free, ready], signal=S("ln_centered"))
            ev = dve(lambda e: e.tensor_copy(centered[:, :], g[:, :]),
                     [ev, last["centered_read"]], signal=S("ln_center_kept"))
            bank_read(i, ev)
            return pool(lambda e: e.tensor_tensor(rstd[:, :], centered[:, :], centered[:, :], ALU.mult),
                        [ev, last["rstd_read"]], signal=S("ln_squared"))

        def norm_var(squared):
            i, g, free = take_bank()
            ev = pe(lambda e: e.matmul(g[:, :], mean, rstd[:, :], start=True, stop=True),
                    [free, squared], signal=S("ln_var"))
            ev = dve(lambda e: e.tensor_scalar(rstd[:, :], g[:, :], EPS, None, ALU.add),
                     [ev], signal=S("ln_var_kept"))
            bank_read(i, ev)
            ev = dve(lambda e: e.transpose(var_t.rearrange("p w k -> p (w k)"), rstd[:, :]),
                     [ev, last["var_t_read"]], signal=S("ln_var_turned"))
            return dve(lambda e: e.reciprocal(var_t[:, :, 0:1], var_t[:, :, 0:1]), [ev], signal=S("ln_inv"))

        def norm_root(inv):
            ev = act(lambda e: e.activation(var_t[:, :, 0:1], var_t[:, :, 0:1], ACT.Sqrt), [inv],
                     signal=S("ln_rstd"))
            ev = dve(lambda e: e.transpose(rstd[:, :], var_t[:, :, 0:1].broadcast_to([P, ITEM_WINS, WIN])),
                     [ev], signal=S("ln_rstd_turned"))
            last["var_t_read"] = ev
            return ev

        def norm_apply(ev, dst, gain=None, bias=None, dst_free=()):
            to = dst if gain is None else centered[:, :]
            ev = pool(lambda e: e.tensor_tensor(to, centered[:, :], rstd[:, :], ALU.mult),
                      [ev, *dst_free], signal=S("ln_scaled"))
            last["rstd_read"] = last["centered_read"] = ev
            if gain is not None:
                ev = pool(lambda e: e.tensor_scalar(dst, centered[:, :], gain, bias, ALU.mult, ALU.add),
                          [ev], signal=S("ln_affine"))
                last["centered_read"] = ev
            return ev

        xs_read = [None] * CHUNKS

        def shift_tokens(c, ready):
            src = x[:, c * COLS:(c + 1) * COLS].rearrange("p (s t) -> p s t", s=CHUNK_SEQS)
            dst = xs[:, c * CHUNK_SEQS:(c + 1) * CHUNK_SEQS, :]
            act(lambda e: e.activation(dst[0:64, :, :], src[0:64, :, :], ACT.Copy),
                [ready, xs_read[c], ev_zero])
            return act(lambda e: e.activation(dst[64:P, :, 1:SEQ], src[64:P, :, 0:SEQ - 1], ACT.Copy),
                       signal=S("shifted_tokens"))

        items = [(layer, c) for layer in range(DEPTH) for c in range(CHUNKS)]
        slot_free = {"wqk": [None] * PAIRS, "raw": [None, None], "wv": [None, None], "sin": [None, None],
                     "wo": None, "w1": None, "w2": None}
        w_ready = {}
        ring_read = [[None] * RING, [None] * RING]
        v_read = [None, None]
        att_read = [ev_bf] * PAIRS
        misc = {"squares": [None] * 4, "partner": [None, None], "proj": [None, None], "xs_parts": [None, None],
                "scores": None, "attp": [None, None], "sums_read": None, "inv_parts_read": None,
                "inv_read": None, "norm_t_read": None,
                "q_scale_read": [None, None], "k_inv_read": None, "probs_read": [None, None], "probs_t_read": [None, None],
                "hidden_read": None}
        vround = {"n": 0}

        def stack(enter):
            state = {}
            x_state = [None] * CHUNKS
            entering = {}

            def load_pair(layer, p):
                r = p % 2
                src = wqkv_in[layer].rearrange("d (k c) -> d k c", k=3)[:, 0:2, p * P:(p + 1) * P]
                raw = wqk_raw[:, r, :]
                ev = sp(lambda e: e.dma_start(raw.rearrange("d (k c) -> d k c", k=2), src),
                        [slot_free["raw"][r]], signal=S(f"wqk_raw{r}_loaded"), by=16)
                slot_free["raw"][r] = split_pair(layer, p, raw, ev)

            def split_pair(layer, p, raw, ev):
                ev_hi = act(lambda e: e.activation(wqk_hi[:, p, :], raw, ACT.Copy), [ev, slot_free["wqk"][p]],
                            signal=S("wqk_hi_made"))
                ev_lo = dve(lambda e: e.tensor_tensor(wqk_lo[:, p, :], raw, wqk_hi[:, p, :].bitcast(F32),
                                                      ALU.subtract), [ev_hi], signal=S("wqk_lo_made"))
                w_ready["wqk", layer, p] = ev_lo
                return ev_lo

            def load_tables(layer):
                for which in range(2):
                    w_ready["sin", layer, which] = pool(
                        lambda e, which=which: e.tensor_scalar(sin_scaled[:, which, :], tables[:, 2 * which + 1, :],
                        vcol(layer, V_QSR + 2 * which), None, ALU.mult),
                        [slot_free["sin"][which], ev_vec, ev_const], signal=S("sin_scaled"))

            def load_v(layer):
                i = vround["n"] % 2
                vround["n"] += 1
                w_ready["wv", layer] = (i, sp(lambda e: e.dma_start(wv[:, i, :], wqkv_in[layer][:, 2 * INNER:]),
                                              [slot_free["wv"][i]], signal=S(f"wv{i}_loaded"), by=16))

            def load_wo(layer):
                src = wo_in[layer].rearrange("(p d) n -> d p n", d=P)
                w_ready["wo", layer] = sp(lambda e: e.dma_start(wo[:, :, :], src), [slot_free["wo"]],
                                          signal=S("wo_loaded"), by=16)

            def load_w1(layer):
                w_ready["w1", layer] = sp(lambda e: e.dma_start(w1[:, :], w1_in[layer]), [slot_free["w1"]],
                                          signal=S("w1_loaded"), by=16)

            def load_w2(layer):
                full = len(HIDDEN_CUTS) - 1
                src = w2_in[layer][0:full * P, :].rearrange("(j d) n -> d j n", d=P)
                sp(lambda e: e.dma_start(w2[:, 0:full, :], src), [slot_free["w2"]],
                   signal=S("w2_loaded"), by=16)
                a, n = HIDDEN_CUTS[-1]
                w_ready["w2", layer] = sp(lambda e: e.dma_start(w2[0:n, full, :], w2_in[layer][a:a + n, :]),
                                          signal=S("w2_loaded"), by=16)

            def vcol(layer, i):
                return vec[:, layer * V_END + i:layer * V_END + i + 1]

            def split_tokens(n):
                c, r = items[n][1], n % 2
                src = xs[:, c * CHUNK_SEQS:(c + 1) * CHUNK_SEQS, :].rearrange("p s t -> p (s t)")
                ev = act(lambda e: e.activation(xs_hi[:, r, :], src, ACT.Copy), [x_state[c], misc["xs_parts"][r]],
                         signal=S("xs_hi_made"))
                state[n]["xs"] = dve(lambda e: e.tensor_tensor(xs_lo[:, r, :], src, xs_hi[:, r, :].bitcast(F32),
                                     ALU.subtract), [ev], signal=S("xs_lo_made"))

            def project(n, p, which):
                layer, r, g = items[n][0], n % 2, proj[which]
                cut = slice(which * P, (which + 1) * P)
                parts = [(wqk_lo, xs_hi), (wqk_hi, xs_lo), (wqk_hi, xs_hi)]
                for j, (w, y) in enumerate(parts):
                    pp = pe(lambda e, j=j, w=w, y=y: e.matmul(g[:, :], w[:, p, cut], y[:, r, :], start=(j == 0),
                            stop=(j == 2)), [state[n]["xs"], w_ready["wqk", layer, p], misc["proj"][which]],
                            signal=S("proj_done") if j == 2 else None)
                slot_free["wqk"][p] = misc["xs_parts"][r] = pp
                sq = (2 * p + which) % 4
                sq_ev = act(lambda e: e.activation(squares[:, sq, :], g[:, :], ACT.Square),
                            [pp, misc["squares"][sq]], signal=S("squared"))
                slot = (n * PAIRS + p) % RING
                y, other = qk_ring[which][:, slot, :], partner[:, which, :]

                def by_seq(a):
                    return a.rearrange("p (s t) -> p s t", s=CHUNK_SEQS)

                def both(a):
                    return a.unsqueeze(1).broadcast_to([P, CHUNK_SEQS, SEQ])

                ra = dve(lambda e: e.stream_shuffle(other, g[:, :], PARTNER), [sq_ev, misc["partner"][which]],
                         signal=S("partnered"))
                rb = dve(lambda e: e.scalar_tensor_tensor(out=by_seq(y), in0=by_seq(g[:, :]),
                         scalar=vcol(layer, V_QS + 2 * which), in1=both(tables[:, 2 * which, :]),
                         op0=ALU.mult, op1=ALU.mult), [ring_read[which][slot], ev_vec, ev_const],
                         signal=S("cos_done"))
                misc["proj"][which] = rb
                rc = pool(lambda e: e.tensor_tensor(by_seq(other), by_seq(other), both(sin_scaled[:, which, :]),
                                                    ALU.mult), [ra, w_ready["sin", layer, which]],
                          signal=S("sin_done"))
                slot_free["sin"][which] = rc
                done = pool(lambda e: e.tensor_tensor(y, y, other, ALU.add), [rb, rc], signal=S("rotated"))
                misc["partner"][which] = done
                state[n]["sq", p, which] = sq_ev
                state[n]["rot", p, which] = done

            def sum_squares(n, couple):
                for j in range(4):
                    p, which = 2 * couple + j // 2, j % 2
                    sel = consts[:, C_SUMSEL + 30 - 2 * couple:C_SUMSEL + 62 - 2 * couple]
                    wait = [state[n]["sq", p, which]]
                    if couple == 0:
                        wait += [misc["sums_read"], ev_const]
                    ev = pe(lambda e, j=j, sel=sel: e.matmul(sums[32 * j:32 * j + 32, :], sel,
                            squares[:, j, :], start=(couple == 0), stop=(couple == PAIRS // 2 - 1)),
                            wait, signal=S("squares_summed") if j == 3 else None)
                misc["squares"] = [ev] * 4
                state[n]["sums"] = ev

            def invert_norms(n):
                ev = dve(lambda e: e.tensor_scalar(inv_norm[:, :], sums[:, :], 1e-24, None, ALU.max),
                         [state[n]["sums"], misc["inv_read"]], signal=S("sums_kept"))
                misc["sums_read"] = ev
                ev = dve(lambda e: e.transpose(norm_t.rearrange("p w h -> p (w h)"), inv_norm[:, :]),
                         [ev, misc["norm_t_read"]], signal=S("sums_turned"))
                used = norm_t[:, :, 0:NORM_ROWS]
                ev = dve(lambda e: e.reciprocal(used, used), [ev], signal=S("sums_inverted"))
                state[n]["inverted"] = ev

            def root_norms(n):
                ev = state[n]["inverted"]
                used = norm_t[:, :, 0:NORM_ROWS]
                for g in range(4):
                    h, r0 = g % 2, 2 * WIN * (g // 2)
                    src = norm_t[r0:r0 + WIN, :, h:NORM_ROWS:2].rearrange("p w g -> p g w")
                    q_ev = act(lambda e, g=g, src=src: e.activation(q_scale8[WIN * g:WIN * g + WIN, n % 2, :, :],
                               src, ACT.Sqrt, scale=QK_SCALE * QK_SCALE), [ev, misc["q_scale_read"][n % 2]],
                               signal=S("q_scaled"))
                state[n]["q_scale"] = q_ev
                state[n]["k_root"] = act(lambda e: e.activation(used, used, ACT.Sqrt), [q_ev],
                                         signal=S("k_norms_inverted"))

            def turn_k_norms(n):
                ev = dve(lambda e: e.transpose(inv_norm[:, :], norm_t.rearrange("p w h -> p (w h)")),
                         [state[n]["k_root"]], signal=S("k_norms_turned"))
                misc["norm_t_read"] = state[n]["k_turned"] = ev

            def split_k_norms(n):
                ev = state[n]["k_turned"]
                ev = act(lambda e: e.activation(inv_hi[:, :], inv_norm[:, :], ACT.Copy),
                                         [ev, misc["inv_parts_read"]], signal=S("inv_hi_made"))
                state[n]["inv"] = misc["inv_read"] = dve(
                    lambda e: e.tensor_tensor(inv_lo[:, :], inv_norm[:, :], inv_hi[:, :].bitcast(F32), ALU.subtract),
                    [ev], signal=S("inv_lo_made"))

            def project_v(n, p):
                layer, c = items[n]
                i, g, free = take_bank()
                wi, wv_ready = w_ready["wv", layer]
                for w in range(2):
                    win = 2 * p + w
                    lhs = xs[:, c * CHUNK_SEQS + win // NWIN, (win % NWIN) * WIN:(win % NWIN + 1) * WIN]
                    for q in range(4):
                        rhs = wv[:, wi, :].rearrange("d (r g c) -> d g r c", g=4, c=DH)[:, q, :, :]
                        o = g[32 * q:32 * q + 32, w * 256:(w + 1) * 256]
                        ev = pe(lambda e, o=o, lhs=lhs, rhs=rhs: e.matmul(o, lhs, rhs, start=True, stop=True),
                                [free, wv_ready, x_state[c]],
                                signal=S("v_projected") if w == 1 and q == 3 else None)
                slot_free["wv"][wi] = ev
                xs_read[c] = ev
                to = v_buf[:, n % 2, 2 * p:2 * p + 2, :]
                ev = act(lambda e: e.activation(to, g[:, :].rearrange("p (w c) -> p w c", w=2), ACT.Copy),
                         [ev, v_read[n % 2]], signal=S("v_kept"))
                bank_read(i, ev)
                state[n]["v", p] = ev

            def spread_k_norms(n, group):
                i, g, free = take_bank()
                sel = spread_sel[:, group * P:(group + 1) * P]
                pe(lambda e: e.matmul(g[:, :], sel, inv_lo[:, :], start=True, stop=False),
                   [free, state[n]["inv"]])
                ev = pe(lambda e: e.matmul(g[:, :], sel, inv_hi[:, :], start=False, stop=True),
                        signal=S("norm_spread"))
                misc["inv_parts_read"] = ev
                ev = dve(lambda e: e.tensor_copy(k_inv[:, WIN:], g[:, :]), [ev, misc["k_inv_read"]],
                         signal=S("k_inv_kept"))
                bank_read(i, ev)
                state[n]["k_inv"] = ev

            def attend_scores(n, s):
                group, seq = s // CHUNK_SEQS, s % CHUNK_SEQS
                pe(lambda e: e.matmul(scores[:, :], ident_bf[:, :], mask_bf[:, :], start=True, stop=False,
                                      skip_group_check=True),
                   [misc["scores"], ev_bf] + [state[n]["rot", 2 * group + j, k] for j in range(2) for k in range(2)])
                for w in range(NWIN):
                    for h in range(4):
                        slot = (n * PAIRS + 2 * group + h // 2) % RING
                        r0 = DH * (h % 2)
                        t0 = seq * SEQ + w * WIN
                        back = WIN if w else 0
                        qw = qk_ring[0][r0:r0 + DH, slot, t0:t0 + WIN]
                        kw = qk_ring[1][r0:r0 + DH, slot, t0 - back:t0 + WIN]
                        o = scores[32 * h:32 * h + 32, w * 2 * WIN + WIN - back:(w + 1) * 2 * WIN]
                        end = w == NWIN - 1 and h == 3
                        ev = pe(lambda e, o=o, qw=qw, kw=kw: e.matmul(o, qw, kw, start=False, stop=True,
                                skip_group_check=True), signal=S("scored") if end else None)
                for j in range(2):
                    slot = (n * PAIRS + 2 * group + j) % RING
                    ring_read[0][slot] = ring_read[1][slot] = ev
                state[n]["scored", s] = ev

            def spread_keys(y):
                return y.unsqueeze(2).broadcast_to([P, NWIN, 2 * WIN])

            def attend_scale(n, s):
                group, seq = s // CHUNK_SEQS, s % CHUNK_SEQS
                b = s % 2
                s3 = scores[:, :].rearrange("p (w k) -> p w k", w=NWIN)

                y3 = probs[:, b, :].rearrange("p (w k) -> p w k", w=NWIN)
                start = k_inv[:, seq * SEQ:seq * SEQ + 1]
                keys = bass.AP(start.tensor, start.offset, [list(start.ap[0]), [WIN, NWIN], [1, 2 * WIN]])
                ev = dve(lambda e: e.tensor_tensor(y3, s3, keys, ALU.mult),
                         [state[n]["scored", s], misc["probs_read"][b], state[n]["k_inv"], ev_ones], signal=S("k_norms_off"))
                misc["scores"] = misc["k_inv_read"] = state[n]["k_scaled", s] = ev

            def attend_max(n, s):
                group, seq = s // CHUNK_SEQS, s % CHUNK_SEQS
                b = s % 2
                y3 = probs[:, b, :].rearrange("p (w k) -> p w k", w=NWIN)
                ev = state[n]["k_scaled", s]
                ev = dve(lambda e: e.tensor_reduce(row_max[:, b, :], y3, AX.X, ALU.max),
                         [ev], signal=S("row_max"))
                ev = dve(lambda e: e.tensor_tensor(y3, y3, spread_keys(row_max[:, b, :]), ALU.subtract),
                         [ev], signal=S("max_off"))
                wins = slice(seq * NWIN, (seq + 1) * NWIN)
                scale = q_scale8[:, n % 2, group, wins]
                state[n]["scaled", s] = misc["q_scale_read"][n % 2] = pool(
                    lambda e: e.tensor_tensor(y3, y3, spread_keys(scale), ALU.mult),
                    [ev, state[n]["q_scale"]], signal=S("q_norms_off"))

            def attend_exp(n, s):
                y = probs[:, s % 2, :]
                state[n]["exp", s] = act(lambda e: e.activation(y, y, ACT.Exp), [state[n]["scaled", s]],
                                         signal=S("exponent"))

            def attend_probs(n, s):
                b = s % 2

                def cube(y):
                    return y.rearrange("p (w k) -> p w k", w=NWIN)

                ev = dve(lambda e: e.tensor_reduce(row_sum[:, b, :], cube(probs[:, b, :]), AX.X, ALU.add),
                         [state[n]["exp", s]], signal=S("row_sum"))
                ev = dve(lambda e: e.reciprocal(row_sum[:, b, :], row_sum[:, b, :]), [ev], signal=S("row_inv"))
                state[n]["p", s] = pool(lambda e: e.tensor_tensor(cube(probs[:, b, :]), cube(probs[:, b, :]),
                                        spread_keys(row_sum[:, b, :]), ALU.mult), [ev], signal=S("probs_done"))

            def attend_turn(n, s):
                b = s % 2
                ev = dve(lambda e: e.transpose(probs_t[:, b, :], probs[:, b, :]),
                         [state[n]["p", s], misc["probs_t_read"][b]], signal=S("probs_turned"))
                misc["probs_read"][b] = ev
                state[n]["pt", s] = ev

            def attend_values(n, s, blocks, done):
                group, seq = s // CHUNK_SEQS, s % CHUNK_SEQS
                b = s % 2
                for kb in blocks:
                    width = 2 * WIN if kb < NWIN - 1 else WIN
                    for h in range(4):
                        lhs = v_buf[32 * h:32 * h + 32, n % 2, seq * NWIN + kb, group * DH:(group + 1) * DH]
                        rhs = probs_t[32 * h:32 * h + 32, b, kb * 64 + WIN:kb * 64 + WIN + width]
                        o = attp[h // 2][DH * (h % 2):DH * (h % 2) + DH, kb * WIN:kb * WIN + width]
                        end = kb == NWIN - 1 and h == 3
                        ev = pe(lambda e, o=o, lhs=lhs, rhs=rhs, kb=kb: e.matmul(o, lhs, rhs, start=(kb == 0),
                                stop=True, skip_group_check=True),
                                [state[n]["pt", s], state[n]["v", (seq + 1) * NWIN // 2 - 1], *misc["attp"]],
                                signal=S("valued") if end else None)
                if not done:
                    return
                misc["probs_t_read"][b] = ev
                v_read[n % 2] = ev
                for j in range(2):
                    to = att[:, 2 * group + j, seq * SEQ:(seq + 1) * SEQ]
                    k = act(lambda e, j=j, to=to: e.activation(to, attp[j][:, 0:SEQ], ACT.Copy),
                            [ev, att_read[2 * group + j]], signal=S("att_kept"))
                    misc["attp"][j] = k
                state[n]["att"] = k

            def project_out(n, pairs):
                layer, c = items[n]
                i, g, free = take_bank()
                for p in pairs:
                    ev = pe(lambda e, p=p: e.matmul(g[:, :], wo[:, p, :], att[:, p, :], start=(p == pairs[0]),
                                                    stop=(p == pairs[-1])),
                            [free, w_ready["wo", layer], state[n]["att"]],
                            signal=S("out_projected") if p == pairs[-1] else None)
                for p in pairs:
                    att_read[p] = ev
                slot_free["wo"] = ev
                xc = x[:, c * COLS:(c + 1) * COLS]
                ev = dve(lambda e: e.tensor_tensor(xc, xc, g[:, :], ALU.add), [ev, x_state[c]],
                         signal=S("att_added"))
                bank_read(i, ev)
                if pairs[-1] < PAIRS - 1:
                    x_state[c] = ev
                    return
                x_state[c] = shift_tokens(c, ev)
                if c == CHUNKS - 1 and layer + 1 < DEPTH:
                    load_wo(layer + 1)

            def ffn_center(n):
                c = items[n][1]
                rhs = xs[:, c * CHUNK_SEQS:(c + 1) * CHUNK_SEQS, :]
                state[n]["lnsq"] = norm_center(rhs, x_state[c])
                xs_read[c] = (S("ln_centered").sem, S("ln_centered").count)

            def ffn_var(n):
                state[n]["lninv"] = norm_var(state[n]["lnsq"])

            def ffn_root(n):
                state[n]["lnroot"] = norm_root(state[n]["lninv"])

            def ffn_norm(n):
                layer = items[n][0]
                state[n]["xn"] = norm_apply(state[n]["lnroot"], centered[:, :], vcol(layer, V_G), vcol(layer, V_B))

            def ffn_gate(n, j):
                layer = items[n][0]
                a, m = HIDDEN_CUTS[j]
                i, g, free = take_bank()
                ev = pe(lambda e: e.matmul(g[0:m, :], w1[:, HIDDEN + a:HIDDEN + a + m], centered[:, :],
                        start=True, stop=True), [free, w_ready["w1", layer], state[n]["xn"]], signal=S("gate_done"))
                ev = act(lambda e: e.activation(hidden[0:m, j, :], g[0:m, :], ACT.Gelu,
                         bias=vcol(layer, V_BG + j)[0:m, :]), [ev, misc["hidden_read"]], signal=S("gelu_done"))
                bank_read(i, ev)
                state[n]["gate", j] = ev

            def ffn_value(n, j):
                layer = items[n][0]
                a, m = HIDDEN_CUTS[j]
                i, g, free = take_bank()
                ev = pe(lambda e: e.matmul(g[0:m, :], w1[:, a:a + m], centered[:, :], start=True, stop=True),
                        [free], signal=S("value_done"))
                last["centered_read"] = slot_free["w1"] = ev
                ev = dve(lambda e: e.scalar_tensor_tensor(out=hidden[0:m, j, :], in0=g[0:m, :],
                         scalar=vcol(layer, V_BA + j)[0:m, :], in1=hidden[0:m, j, :], op0=ALU.add, op1=ALU.mult),
                         [ev, state[n]["gate", j]], signal=S("hidden_done"))
                bank_read(i, ev)
                state[n]["hidden"] = ev
                if j == len(HIDDEN_CUTS) - 1 and items[n][1] == CHUNKS - 1 and layer + 1 < DEPTH:
                    load_w1(layer + 1)

            def ffn_out(n):
                layer, c = items[n]
                i, g, free = take_bank()
                for j, (a, m) in enumerate(HIDDEN_CUTS):
                    ev = pe(lambda e, j=j, m=m: e.matmul(g[:, :], w2[0:m, j, :], hidden[0:m, j, :],
                            start=(j == 0), stop=(j == len(HIDDEN_CUTS) - 1)),
                            [free, w_ready["w2", layer], state[n]["hidden"]],
                            signal=S("ffn_done") if j == len(HIDDEN_CUTS) - 1 else None)
                misc["hidden_read"] = slot_free["w2"] = ev
                xc = x[:, c * COLS:(c + 1) * COLS]
                ev = dve(lambda e: e.scalar_tensor_tensor(out=xc, in0=g[:, :], scalar=vcol(layer, V_B2), in1=xc,
                         op0=ALU.add, op1=ALU.add), [ev, x_state[c]], signal=S("ffn_added"))
                bank_read(i, ev)
                x_state[c] = shift_tokens(c, ev)
                if c == CHUNKS - 1 and layer + 1 < DEPTH:
                    load_w2(layer + 1)

            first_raw = att[:, PAIRS // 2:, :].rearrange("p a (b c) -> p (a b) c", c=2 * P)
            src = wqkv_in[0].rearrange("d (k p c) -> d k p c", k=3, c=P)
            for k in range(2):
                ev_first = sp(lambda e, k=k: e.dma_start(first_raw[:, :, k * P:(k + 1) * P], src[:, k, :, :]),
                              signal=S("wqk_first_loaded"), by=16)
            load_v(0)
            for x_state[0] in enter(0):
                pass
            load_tables(0)
            for p in range(2):
                split_pair(0, p, first_raw[:, p, :], ev_first)
            load_wo(0)
            load_w1(0)
            load_w2(0)
            N = len(items)
            early = {4: [lambda n: project_out(n, (4, 5, 6, 7))], 5: [ffn_center],
                     7: [ffn_root, ffn_norm], 11: [ffn_out]}
            late = {8 + j: [lambda n, j=j: ffn_gate(n, j), lambda n, j=j: ffn_value(n, j)]
                    for j in range(len(HIDDEN_CUTS))}
            after_k = {-3: [lambda n: project_out(n, (0, 1))], -1: [lambda n: project_out(n, (2, 3))]}
            end = {6: [ffn_var]}

            def stage_c(t, pieces):
                for k, stages in pieces.items():
                    n = (t - k) // SUBSTEPS - 2
                    if (t - k) % SUBSTEPS == 0 and 0 <= n < N:
                        for stage in stages:
                            stage(n)

            def at(t, lag):
                n, p = divmod(t - lag, SUBSTEPS)
                return (n, p) if 0 <= n < N else None

            for t in range(SUBSTEPS * (N + 3) + 6):
                n, p = divmod(t, SUBSTEPS)
                now = at(t, 0)
                if p == 0 and now and n and items[n][1] == 0:
                    load_tables(items[n][0])
                stage_c(t, early)
                norms_due = p == 1 and 0 <= n - 1 < N
                if norms_due:
                    invert_norms(n - 1)
                if scores_at := at(t, SCORES_LAG):
                    attend_scores(*scores_at)
                if p % 2 == 0:
                    m, couple = (n, p // 2 - 1) if p else (n - 1, PAIRS // 2 - 1)
                    if 0 <= m < N and couple >= 0:
                        sum_squares(m, couple)
                if now:
                    if t == 0:
                        state[0] = {}
                        split_tokens(0)
                    project(n, p, 0)
                if scores_at and p % 2 == 0:
                    spread_k_norms(scores_at[0], scores_at[1] // 2)
                if v_at := at(t, V_LAG):
                    project_v(*v_at)
                if norms_due:
                    root_norms(n - 1)
                if scores_at:
                    attend_scale(*scores_at)
                if probs_at := at(t, PROBS_LAG):
                    attend_probs(*probs_at)
                if scores_at:
                    attend_max(*scores_at)
                if norms_due:
                    turn_k_norms(n - 1)
                if values_at := at(t, VALUES_LAG):
                    attend_values(*values_at, range(0, NWIN // 2), False)
                stage_c(t, late)
                if values_at:
                    attend_values(*values_at, range(NWIN // 2, NWIN), True)
                if norms_due:
                    split_k_norms(n - 1)
                if now:
                    project(n, p, 1)
                stage_c(t, after_k)
                if probs_at:
                    attend_turn(*probs_at)
                if scores_at:
                    attend_exp(*scores_at)
                stage_c(t, end)
                if now:
                    layer, c = items[n]
                    if c == CHUNKS - 1 and layer + 1 < DEPTH:
                        load_pair(layer + 1, p)
                        if p == 0:
                            load_v(layer + 1)
                if n == 0 and p + 2 < PAIRS:
                    att_read[PAIRS // 2:] = [split_pair(0, p + 2, first_raw[:, p + 2, :], ev_first)] * (PAIRS // 2)
                if n + 1 < CHUNKS and p in (2, 3, 4):
                    if p == 2:
                        entering = enter(n + 1)
                    x_state[n + 1] = next(entering)
                if now and n < N - 1 and p == SUBSTEPS - 2:
                    state[n + 1] = {}
                    split_tokens(n + 1)
            return x_state

        def half_step(ready):
            stored = [sp(lambda e, c=c: e.dma_start(base_dram[:, c * COLS:(c + 1) * COLS],
                      x[:, c * COLS:(c + 1) * COLS]), [ready[c]], signal=S(f"base{c}_stored"), by=16)
                      for c in range(CHUNKS)]

            def enter(c):
                xc = x[:, c * COLS:(c + 1) * COLS]
                sq = norm_center(xc, ready[c])
                yield None
                var = norm_var(sq)
                yield None
                ev = norm_apply(norm_root(var), xc, dst_free=[stored[c]])
                yield shift_tokens(c, ev)

            ends = stack(enter)
            done = []
            for c in range(CHUNKS):
                base = qk_ring[0][:, c, :]
                ev = sp(lambda e, c=c, base=base: e.dma_start(base, base_dram[:, c * COLS:(c + 1) * COLS]),
                        [stored[c], *ring_read[0]], signal=S(f"base{c}_loaded"), by=16)
                xc = x[:, c * COLS:(c + 1) * COLS]
                done.append(dve(lambda e, xc=xc, base=base: e.scalar_tensor_tensor(out=xc, in0=xc, scalar=0.5,
                            in1=base, op0=ALU.mult, op1=ALU.add), [ev, ends[c]], signal=S("half_added")))
                for w in (0, 1):
                    ring_read[w] = [done[-1]] * RING
            return done

        def scan_block():
            barrier()
            tiles = [qk_ring[k][:, i, :] for k in (0, 1) for i in range(RING)]
            xn, z, e1, ln1, corr, y = tiles[0:6]
            u, dt, dtu, gate = tiles[6:8], tiles[8:10], tiles[10:12], tiles[12:14]
            decay, drive, hstate, hc, c_kept = (tiles[14 + 2 * k:16 + 2 * k] for k in range(5))
            bc_hi = [wqk_hi[:, k:k + 2, :].rearrange("p a c -> p (a c)") for k in (1, 3)]
            bc_lo = [wqk_lo[:, k:k + 2, :].rearrange("p a c -> p (a c)") for k in (1, 3)]
            row_sel = wqk_hi[:, 0, 0:2 * STATES]
            b_bank, c_bank, acc_bank = proj, attp, [scores, sums]
            padded = v_buf[:, 0, 0:3, :].rearrange("p w c -> p (w c)")[:, 0:CHUNK_SEQS * (SEQ + 2)]\
                .rearrange("p (s t) -> p s t", s=CHUNK_SEQS)
            mw = v_buf[:, 1, 0:2, :].rearrange("p w c -> p (w c)").rearrange("p (m n) -> p m n", m=4)
            wbc = v_buf[:, 1, 2, 0:P]
            mvec = v_buf[:, 1, 3, 0:M_END]
            neg_a = v_buf[:, 1, 4, 0:STATES]

            def mcol(i):
                return mvec[:, i:i + 1]

            sp(lambda e: e.dma_start(mw, mw_in.rearrange("m d n -> d m n")), signal=S("m_loaded"), by=16)
            sp(lambda e: e.dma_start(wbc, wb_in), signal=S("m_loaded"), by=16)
            ev_m = sp(lambda e: e.dma_start(mvec, mvec_in), signal=S("m_loaded"), by=16)
            ev = act(lambda e: e.activation(neg_a, mvec[:, M_ALOG:M_ALOG + STATES], ACT.Exp), [ev_m],
                     signal=S("m_a"))
            ev_a = act(lambda e: e.mul(neg_a, neg_a, -1.0), [ev], signal=S("m_a"))
            ev_pad = pool(lambda e: e.memset(padded, 0.0), signal=S("m_pad"))
            ev_sel = dve(lambda e: e.tensor_copy(row_sel, ident[:, 0:2 * STATES]), signal=S("m_sel"))
            rd = {k: [None, None] for k in ("decay", "drive", "h", "hc", "c_kept", "b_bank", "c_bank", "acc", "u",
                                            "dt", "dtu", "gate", "bc")}
            rd["xn"] = rd["y"] = None
            made = {}
            done = [None] * CHUNKS
            chain = S("m_dve")

            def D(make, after=()):
                return dve(make, [*after, (chain.sem, chain.count)] if chain.count else after, signal=chain)

            def linear(m, rhs, waits):
                i, g, free = take_bank()
                return i, g, pe(lambda e: e.matmul(g[:, :], mw[:, m, :], rhs, start=True, stop=True),
                                [free, ev_m, *waits], signal=S("m_linear"))

            def prepare(c):
                k = c % 2
                xc = x[:, c * COLS:(c + 1) * COLS]
                ev = rd["xn"]
                for gain, bias in ((None, None), (mcol(M_G), mcol(M_B))):
                    sq = norm_center(xc if gain is None else xn, ev)
                    yield
                    var = norm_var(sq)
                    yield
                    ev = norm_apply(norm_root(var), xn, gain, bias, dst_free=[rd["xn"]])
                    yield
                ev_xn = ev
                i, g, ev = linear(0, xn, [ev_xn])
                g3 = g[:, :].rearrange("p (s t) -> p s t", s=CHUNK_SEQS)
                yield
                ev = D(lambda e: e.tensor_scalar(padded[:, :, 1:SEQ + 1], g3, mcol(M_W1B), None, ALU.add),
                       [ev, ev_pad])
                bank_read(i, ev)
                i, g, ev = linear(1, xn, [ev_xn])
                rd["xn"] = ev
                ev_gate = act(lambda e, g=g: e.activation(gate[k], g[:, :], ACT.Silu, bias=mcol(M_V1B)),
                              [ev, rd["gate"][k]], signal=S("m_gate"))
                bank_read(i, ev_gate)
                yield
                u3 = u[k].rearrange("p (s t) -> p s t", s=CHUNK_SEQS)
                D(lambda e: e.tensor_scalar(u3, padded[:, :, 0:SEQ], mcol(M_CONV), None, ALU.mult),
                  [ev_m, rd["u"][k]])
                D(lambda e: e.scalar_tensor_tensor(out=u3, in0=padded[:, :, 1:SEQ + 1], scalar=mcol(M_CONV + 1),
                  in1=u3, op0=ALU.mult, op1=ALU.add))
                ev = D(lambda e: e.scalar_tensor_tensor(out=u3, in0=padded[:, :, 2:SEQ + 2], scalar=mcol(M_CONV + 2),
                       in1=u3, op0=ALU.mult, op1=ALU.add))
                ev_u = act(lambda e: e.activation(u[k], u[k], ACT.Silu), [ev], signal=S("m_u"))
                yield
                i, g, ev_z = linear(2, u[k], [ev_u])
                j, g2, free = take_bank()
                ev = pe(lambda e: e.matmul(g2[:, :], wbc, u[k], start=True, stop=True), [free], signal=S("m_bc"))
                yield
                ev_z = D(lambda e, g=g: e.tensor_scalar(z, g[:, :], mcol(M_BDT), None, ALU.add), [ev_z])
                bank_read(i, ev_z)
                ev_e = D(lambda e: e.scalar_tensor_tensor(out=e1, in0=z, scalar=-1.0, in1=z, op0=ALU.mult,
                         op1=ALU.min))
                ev_e = act(lambda e: e.activation(e1, e1, ACT.Exp), [ev_e], signal=S("m_exp"))
                ev = act(lambda e: e.activation(bc_hi[k], g2[:, :], ACT.Copy), [ev, rd["bc"][k]],
                         signal=S("m_bc_hi"))
                yield
                ev = D(lambda e: e.tensor_tensor(bc_lo[k], g2[:, :], bc_hi[k].bitcast(F32), ALU.subtract), [ev])
                bank_read(j, ev)
                made["bc", c] = ev
                ev = D(lambda e: e.tensor_scalar(corr, e1, 1.0, None, ALU.add), [ev_e])
                ev = act(lambda e: e.activation(ln1, corr, ACT.Ln), [ev], signal=S("m_ln"))
                yield
                D(lambda e: e.scalar_tensor_tensor(out=corr, in0=corr, scalar=1.0, in1=e1, op0=ALU.subtract,
                  op1=ALU.subtract), [ev])
                D(lambda e: e.tensor_tensor(ln1, ln1, corr, ALU.subtract))
                yield
                made["dt", c] = D(lambda e: e.scalar_tensor_tensor(out=dt[k], in0=z, scalar=0.0, in1=ln1,
                                  op0=ALU.max, op1=ALU.add), [rd["dt"][k]])
                made["dtu", c] = D(lambda e: e.tensor_tensor(dtu[k], dt[k], u[k], ALU.mult), [rd["dtu"][k]])
                made["gate", c] = ev_gate

            def finish(c):
                k = c % 2
                xc = x[:, c * COLS:(c + 1) * COLS]
                yield
                yield
                ev = D(lambda e: e.scalar_tensor_tensor(out=y, in0=u[k], scalar=mcol(M_D), in1=acc_bank[k][:, :],
                       op0=ALU.mult, op1=ALU.add), [made["acc", c], rd["y"]])
                rd["acc"][k] = rd["u"][k] = ev
                ev = D(lambda e: e.tensor_tensor(y, y, gate[k], ALU.mult), [made["gate", c]])
                rd["gate"][k] = ev
                i, g, ev = linear(3, y, [ev])
                rd["y"] = ev
                yield
                done[c] = D(lambda e: e.scalar_tensor_tensor(out=xc, in0=g[:, :], scalar=mcol(M_W2B), in1=xc,
                            op0=ALU.add, op1=ALU.add), [ev])
                bank_read(i, done[c])

            def spread_row(g, row, k, waits, signal):
                sel = row_sel[:, row:row + 1].broadcast_to([P, P])
                pe(lambda e: e.matmul(g[:, :], sel, bc_lo[k], start=True, stop=False), [ev_sel, *waits])
                return pe(lambda e: e.matmul(g[:, :], sel, bc_hi[k], start=False, stop=True), signal=signal)

            for step in prepare(0):
                pass
            for c in range(CHUNKS):
                k = c % 2
                beside = []
                if c:
                    beside.append(finish(c - 1))
                if c + 1 < CHUNKS:
                    beside.append(prepare(c + 1))

                def add_state(s):
                    b = s % 2
                    rd["hc"][b] = made["acc", c] = pe(
                        lambda e, k=k: e.matmul(acc_bank[k][:, :], ident, hc[b], start=(s == 0), stop=(s == STATES - 1)),
                        [made["hc", s], rd["acc"][k]], signal=S("m_acc"))

                for s in range(STATES):
                    b = s % 2
                    ev_b = spread_row(b_bank[b], s, k, [made["bc", c], rd["b_bank"][b]], S("m_b"))
                    ev_c = spread_row(c_bank[b], STATES + s, k, [rd["c_bank"][b]], S("m_c"))
                    rd["bc"][k] = ev_c
                    if s >= 2:
                        add_state(s - 2)
                    ev_dec = act(lambda e, s=s, b=b, k=k: e.activation(decay[b], dt[k], ACT.Exp, scale=neg_a[:, s:s + 1]),
                                 [made["dt", c], ev_a, rd["decay"][b]], signal=S("m_decay"))
                    rd["dt"][k] = ev_dec
                    ev = dve(lambda e, b=b, k=k: e.tensor_tensor(drive[b], dtu[k], b_bank[b][:, :], ALU.mult),
                             [ev_b, made["dtu", c], rd["drive"][b]], signal=S("m_drive"))
                    rd["b_bank"][b] = rd["dtu"][k] = ev
                    for q in range(CHUNK_SEQS):
                        cut = slice(q * SEQ, (q + 1) * SEQ)
                        ev_h = dve(lambda e, b=b, cut=cut: e.tensor_tensor_scan(hstate[b][:, cut], decay[b][:, cut],
                                   drive[b][:, cut], 0.0, ALU.mult, ALU.add), [ev, ev_dec, rd["h"][b]],
                                   signal=S("m_scan"))
                    rd["decay"][b] = rd["drive"][b] = ev_h
                    ev = act(lambda e, b=b: e.activation(c_kept[b], c_bank[b][:, :], ACT.Copy),
                             [ev_c, rd["c_kept"][b]], signal=S("m_c_kept"))
                    rd["c_bank"][b] = ev
                    ev = pool(lambda e, b=b: e.tensor_tensor(hc[b], hstate[b], c_kept[b], ALU.mult),
                              [ev, ev_h, rd["hc"][b]], signal=S("m_hc"))
                    rd["h"][b] = rd["c_kept"][b] = made["hc", s] = ev
                    if beside and next(beside[0], "end") == "end":
                        beside.pop(0)
                add_state(STATES - 2)
                add_state(STATES - 1)
                for rest in beside:
                    for step in rest:
                        pass
            for step in finish(CHUNKS - 1):
                pass
            barrier()
            return done

        ready = half_step(x_ready)
        ready = scan_block()
        ready = half_step(ready)

        barrier()
        out_tiles = out.rearrange("b (h p) d -> p (b h) d", p=P)
        stage_out = qk_ring[1][:, 0:4, :].rearrange("p r (h d) -> p (r h) d", d=P)
        for c in range(CHUNKS):
            i, g, free = take_bank()
            for j in range(4):
                ev = pe(lambda e, c=c, j=j, g=g: e.transpose(g[:, j * P:(j + 1) * P],
                        x[:, (4 * c + j) * P:(4 * c + j + 1) * P], ident), [free, ready[c]],
                        signal=S("out_turned") if j == 3 else None)
            ev = dve(lambda e, c=c, g=g: e.tensor_copy(stage_out[:, 4 * c:4 * c + 4, :],
                     g[:, :].rearrange("p (h d) -> p h d", d=P)), [ev], signal=S("out_kept"))
            bank_read(i, ev)
            ev_out = sp(lambda e, c=c: e.dma_start(out_tiles[:, 4 * c:4 * c + 4, :], stage_out[:, 4 * c:4 * c + 4, :]),
                        [ev], signal=S("out_stored"), by=16)
        sp(None, [ev_out])

        block = ctx.enter_context(nc.Block())

        @block.sync
        def _(e):
            sp.run(e)

        @block.tensor
        def _(e):
            pe.run(e)

        @block.vector
        def _(e):
            dve.run(e)

        @block.scalar
        def _(e):
            act.run(e)

        @block.gpsimd
        def _(e):
            pool.run(e)


def constants():
    f = np.float32
    c = np.zeros((P, C_END), f)
    c[:, C_IDENT:C_IDENT + P] = np.eye(P, dtype=f)
    c[:, C_CENTER:C_CENTER + P] = np.eye(P, dtype=f) - f(1 / P)
    c[:, C_MEAN] = f(1 / P)
    c[np.arange(P), C_SUMSEL + 30 + np.arange(P) // DH] = 1
    half = np.arange(0, DH, 2, dtype=f)
    inv_freq = (f(1) / f(10000) ** (half / f(DH))).astype(f)
    t = np.arange(SEQ, dtype=f)
    freqs = t[:, None] * inv_freq[None, :]
    freqs = np.concatenate([freqs, freqs], -1)
    base = ((half + f(0.4 * DH)) / f(1.4 * DH)).astype(f)
    power = ((t - SEQ // 2) / f(WIN // 2)).astype(f)
    scale = base[None, :] ** power[:, None]
    scale = np.concatenate([scale, scale], -1).astype(f)
    inv = (f(1) / scale).astype(f)
    sign = np.where(np.arange(DH) < DH // 2, f(-1), f(1))
    tables = [np.cos(freqs) * scale, np.sin(freqs) * scale * sign, np.cos(freqs) * inv, np.sin(freqs) * inv * sign]
    for i, y in enumerate(tables):
        c[:, C_TABLES + i * SEQ:C_TABLES + (i + 1) * SEQ] = np.tile(y.T[HEAD_ORDER].astype(f), (2, 1))
    i = np.arange(P)[:, None, None] % WIN
    w = np.arange(NWIN)[None, :, None]
    j = np.arange(2 * WIN)[None, None, :]
    seen = np.where(j < WIN, (j >= i) & (w > 0), j - WIN <= i)
    c[:, C_MASK:C_SPREAD] = np.where(seen, f(0), f(-1e30)).reshape(P, -1)
    for head in range(HEADS):
        c[norm_row(head // 2, 1) + head % 2, C_SPREAD + head * WIN:C_SPREAD + (head + 1) * WIN] = 1
    return c


def kernel(**inputs):
    import concourse.bacc as bacc
    from concourse.bass_utils import run_bass_kernel_spmd

    a = {k: np.ascontiguousarray(v) for k, v in inputs.items()}
    vec = np.zeros((P, DEPTH, V_END), np.float32)
    for at, name in ((V_QS, "q_scale"), (V_KS, "k_scale")):
        s = a["L0_ffn_" + name]
        swapped = np.concatenate([s[:, DH // 2:], s[:, :DH // 2]], 1)
        vec[:, :, at] = np.concatenate([s[:, HEAD_ORDER]] * 2, 1).T
        vec[:, :, at + 1] = np.concatenate([swapped[:, HEAD_ORDER]] * 2, 1).T
    vec[:, :, V_G], vec[:, :, V_B], vec[:, :, V_B2] = a["L0_ffn_ln_g"].T, a["L0_ffn_ln_b"].T, a["L0_ffn_b2"].T
    for j, (s, n) in enumerate(HIDDEN_CUTS):
        vec[:n, :, V_BA + j] = a["L0_ffn_b1"][:, s:s + n].T
        vec[:n, :, V_BG + j] = a["L0_ffn_b1"][:, HIDDEN + s:HIDDEN + s + n].T
    m = "L0_attn_"
    mvec = np.concatenate([np.stack([a[m + k] for k in ("ln_g", "ln_b", "w1_b", "v1_b", "w2_b", "D_skip", "b_dt")], 1),
                           a[m + "conv_w"][:, 0, :], a[m + "A_log"]], 1)
    wqkv = a["L0_ffn_Wqkv"].reshape(DEPTH, P, 3, HEADS, DH)
    wqkv = np.concatenate([wqkv[:, :, 0:2][..., HEAD_ORDER], wqkv[:, :, 2:3]], 2).reshape(DEPTH, P, 3 * INNER)
    arrays = {
        "x": a[m + "x"], "consts": constants(), "vec": vec.reshape(P, -1), "mvec": np.ascontiguousarray(mvec),
        "wqkv": wqkv, "wo": a["L0_ffn_Wo"], "w1": a["L0_ffn_W1"], "w2": a["L0_ffn_W2"],
        "mw": np.stack([a[m + k] for k in ("w1_w", "v1_w", "W_dt", "w2_w")]),
        "wb": np.ascontiguousarray(np.concatenate([a[m + "W_B"], a[m + "W_C"]] * (P // (2 * STATES)), 1)),
    }
    nc = bacc.Bacc("TRN2", target_bir_lowering=False, num_devices=1)
    args = [nc.dram_tensor(f"in_{k}", v.shape, mybir.dt.from_np(v.dtype), kind="ExternalInput").ap() for k, v in arrays.items()]
    out = nc.dram_tensor("out", a[m + "x"].shape, F32, kind="ExternalOutput").ap()
    macaron_kernel(nc, *args, out)
    r = run_bass_kernel_spmd(nc, [{f"in_{k}": v for k, v in arrays.items()}], core_ids=[0])
    return r.results[0]["out"]
```
